# Optimizing a Trainium2 kernel written in Bass

```python
import numpy as np
import jax
import jax.numpy as jnp

def _softmax(x, axis=-1):
    return jax.nn.softmax(x, axis=axis)
def _gelu(x):
    return jax.nn.gelu(x, approximate=True)
def _silu(x):
    return jax.nn.silu(x)
def _sigmoid(x):
    return jax.nn.sigmoid(x)
def _layernorm(x, axis=-1, eps=1e-5):
    m = jnp.mean(x, axis=axis, keepdims=True)
    v = jnp.var(x, axis=axis, keepdims=True)
    return (x - m) / jnp.sqrt(v + eps)
def _scatter_add(tgt, idx, src, axis=0):
    return tgt.at[idx].add(src)
def _segment_sum(src, seg, n):
    return jax.ops.segment_sum(src, seg, n)

kernel_name = 'mk_vit_tower_cls_d2_tok_img256_a96439'

def setup_inputs(seed: int = 0):
    np.random.seed(seed)
    _w = jnp.asarray
    def _rec_inputs():
        import jax
        import jax.numpy as jnp
        _rk = jax.random.key(seed)
        x = (-0.000520686 + 1.00062 * jax.random.normal(jax.random.fold_in(_rk, 1), (32, 256, 256, 4), jnp.float32))
        cls_tok = 0.02 * jax.random.normal(jax.random.fold_in(_rk, 5), (1, 1, 256), jnp.float32)
        return x, cls_tok
    x, cls_tok = _rec_inputs()
    def _L0_tok_setup():
        import jax, jax.numpy as jnp
        import numpy as np
        HIDDEN_DIM = 512
        key = jax.random.key(seed)
        k_geom, k_w, k_b = jax.random.split(key, 3)
        B, N, F = (8, 256, 4)
        geom = jax.random.normal(k_geom, (B, N, N, F), dtype=jnp.float32)
        bound = 1.0 / np.sqrt(F)
        W = jax.random.uniform(k_w, (HIDDEN_DIM, F), dtype=jnp.float32, minval=-bound, maxval=bound)
        b = jax.random.uniform(k_b, (HIDDEN_DIM,), dtype=jnp.float32, minval=-bound, maxval=bound)
        return {'geom': geom, 'W': W, 'b': b}
    _L0_tok_all = _L0_tok_setup()
    _L0_tok_in = {k: v for k, v in _L0_tok_all.items() if k in ('W', 'b', )}
    del _L0_tok_all

    def _L0_attn_setup():
        import jax, jax.numpy as jnp
        import numpy as np
        B_, S_, DM, DI, N_, R_, K_ = (2, 2048, 256, 512, 16, 32, 4)
        NB = 4

        def _layer_norm(x, g, b, eps=1e-05):
            m = jnp.mean(x, axis=-1, keepdims=True)
            v = jnp.mean(jnp.square(x - m), axis=-1, keepdims=True)
            return (x - m) * jax.lax.rsqrt(v + eps) * g + b

        def _ssm_scan(dA, dBx, C):

            def step(h, inp):
                dA_t, dBx_t, C_t = inp
                h = dA_t * h + dBx_t
                y = jnp.einsum('bdn,bn->bd', h, C_t)
                return (h, y)
            h0 = jnp.zeros(dA.shape[:1] + dA.shape[2:], dA.dtype)
            _, ys = jax.lax.scan(step, h0, (dA.transpose(1, 0, 2, 3), dBx.transpose(1, 0, 2, 3), C.transpose(1, 0, 2)))
            return ys.transpose(1, 0, 2)

        def _mamba_block(x, in_w, conv_w, conv_b, A_log, xd_w, xB_w, xC_w, dtp_w, dtp_b, D, out_w, g, b):
            res = x
            xn = _layer_norm(x, g, b)
            xz = xn @ in_w
            xs, z = jnp.split(xz, 2, axis=-1)
            xc = jax.lax.conv_general_dilated(xs.transpose(0, 2, 1), conv_w[:, None, :], (1,), [(K_ - 1, 0)], dimension_numbers=('NCH', 'OIH', 'NCH'), feature_group_count=DI)
            xc = jax.nn.silu((xc + conv_b[None, :, None]).transpose(0, 2, 1))
            delta = jax.nn.softplus(xc @ xd_w @ dtp_w + dtp_b)
            Bm = xc @ xB_w
            Cm = xc @ xC_w
            A = -jnp.exp(A_log)
            dA = jnp.exp(delta[..., None] * A)
            dBx = (delta * xc)[..., None] * Bm[:, :, None, :]
            y = _ssm_scan(dA, dBx, Cm) + D * xc
            return y * jax.nn.silu(z) @ out_w + res
        key = jax.random.key(seed)
        ks = jax.random.split(key, 16)

        def rn(k, shape, s=0.02):
            return jax.random.normal(k, shape, jnp.float32) * s
        A = jnp.log(jnp.arange(1, N_ + 1, dtype=jnp.float32))
        return {'x': jax.random.normal(ks[0], (B_, S_, DM), jnp.float32), 'in_w': rn(ks[1], (NB, DM, 2 * DI)), 'conv_w': rn(ks[2], (NB, DI, K_), 0.3), 'conv_b': jnp.zeros((NB, DI), jnp.float32), 'A_log': jnp.broadcast_to(A, (NB, DI, N_)) + 0.0, 'xd_w': rn(ks[3], (NB, DI, R_)), 'xB_w': rn(ks[4], (NB, DI, N_)), 'xC_w': rn(ks[5], (NB, DI, N_)), 'dtp_w': rn(ks[6], (NB, R_, DI), R_ ** (-0.5)), 'dtp_b': jax.random.uniform(ks[7], (NB, DI), jnp.float32, minval=jnp.log(0.001), maxval=jnp.log(0.1)), 'D': jnp.ones((NB, DI), jnp.float32), 'out_w': rn(ks[8], (NB, DI, DM)), 'ln_g': jnp.ones((NB, DM), jnp.float32), 'ln_b': jnp.zeros((NB, DM), jnp.float32), 'merge_w': rn(ks[9], (2 * DM, DM))}
    _L0_attn_all = _L0_attn_setup()
    _L0_attn_in = {k: v for k, v in _L0_attn_all.items() if k in ('in_w', 'conv_w', 'conv_b', 'A_log', 'xd_w', 'xB_w', 'xC_w', 'dtp_w', 'dtp_b', 'D', 'out_w', 'ln_g', 'ln_b', 'merge_w', )}
    del _L0_attn_all

    def _L0_ffn_setup():
        import jax, jax.numpy as jnp
        import numpy as np
        B, A = (4096, 8)
        IN, OUT = (256, 256)
        SH1, SH2 = (256, 128)
        EH1, EH2 = (128, 64)
        E, TOPK = (4, 2)

        def _shared_mlp(x, W1, b1, W2, b2, W3, b3):
            h = jax.nn.relu(x @ W1 + b1)
            h = jax.nn.relu(h @ W2 + b2)
            return h @ W3 + b3

        def _experts_mlp(x, eW1, eb1, eW2, eb2, eW3, eb3):
            h = jax.nn.relu(jnp.einsum('baf,efh->ebah', x, eW1) + eb1[:, None, None, :])
            h = jax.nn.relu(jnp.einsum('ebah,ehg->ebag', h, eW2) + eb2[:, None, None, :])
            o = jnp.einsum('ebag,ego->ebao', h, eW3) + eb3[:, None, None, :]
            return jnp.moveaxis(o, 0, -1)
        key = jax.random.key(seed)
        ks = jax.random.split(key, 16)
        s = 0.05
        return {'x': jax.random.normal(ks[0], (B, A, IN), jnp.float32), 'sW1': jax.random.normal(ks[1], (IN, SH1), jnp.float32) * s, 'sb1': jnp.zeros((SH1,), jnp.float32), 'sW2': jax.random.normal(ks[2], (SH1, SH2), jnp.float32) * s, 'sb2': jnp.zeros((SH2,), jnp.float32), 'sW3': jax.random.normal(ks[3], (SH2, OUT), jnp.float32) * s, 'sb3': jnp.zeros((OUT,), jnp.float32), 'eW1': jax.random.normal(ks[4], (E, IN, EH1), jnp.float32) * s, 'eb1': jnp.zeros((E, EH1), jnp.float32), 'eW2': jax.random.normal(ks[5], (E, EH1, EH2), jnp.float32) * s, 'eb2': jnp.zeros((E, EH2), jnp.float32), 'eW3': jax.random.normal(ks[6], (E, EH2, OUT), jnp.float32) * s, 'eb3': jnp.zeros((E, OUT), jnp.float32), 'gW': jax.random.normal(ks[7], (IN, E), jnp.float32) * s, 'gb': jnp.zeros((E,), jnp.float32)}
    _L0_ffn_all = _L0_ffn_setup()
    _L0_ffn_in = {k: v for k, v in _L0_ffn_all.items() if k in ('sW1', 'sb1', 'sW2', 'sb2', 'sW3', 'sb3', 'eW1', 'eb1', 'eW2', 'eb2', 'eW3', 'eb3', 'gW', 'gb', )}
    del _L0_ffn_all

    def _L1_attn_setup():
        import jax, jax.numpy as jnp
        import numpy as np
        B, N, D = (8, 2048, 256)
        key = jax.random.key(seed)
        k1, k2, k3, k4 = jax.random.split(key, 4)
        s = D ** (-0.5)
        return {'x': jax.random.normal(k1, (B, N, D), dtype=jnp.float32), 'Wq': jax.random.normal(k2, (D, D), dtype=jnp.float32) * s, 'Wk': jax.random.normal(k3, (D, D), dtype=jnp.float32) * s, 'Wv': jax.random.normal(k4, (D, D), dtype=jnp.float32) * s}
    _L1_attn_all = _L1_attn_setup()
    _L1_attn_in = {k: v for k, v in _L1_attn_all.items() if k in ('Wq', 'Wk', 'Wv', )}
    del _L1_attn_all

    def _L1_ffn_setup():
        import jax, jax.numpy as jnp
        import numpy as np
        B, S, D = (8, 4096, 256)
        H = 4 * D
        CAPACITY = 0.5
        key = jax.random.key(seed)
        ks = jax.random.split(key, 6)
        x = jax.random.normal(ks[0], (B, S, D), dtype=jnp.float32)
        attention_mask = jnp.zeros((B, 1, 1, S), dtype=jnp.float32)
        wr = jax.random.normal(ks[1], (D, 1), dtype=jnp.float32) * 0.02
        br = jnp.zeros((1,), dtype=jnp.float32)
        w1 = jax.random.normal(ks[2], (D, H), dtype=jnp.float32) * 0.02
        b1 = jnp.zeros((H,), dtype=jnp.float32)
        w2 = jax.random.normal(ks[3], (H, D), dtype=jnp.float32) * 0.02
        b2 = jnp.zeros((D,), dtype=jnp.float32)
        return {'x': x, 'attention_mask': attention_mask, 'wr': wr, 'br': br, 'w1': w1, 'b1': b1, 'w2': w2, 'b2': b2}
    _L1_ffn_all = _L1_ffn_setup()
    _L1_ffn_in = {k: v for k, v in _L1_ffn_all.items() if k in ('attention_mask', 'wr', 'br', 'w1', 'b1', 'w2', 'b2', )}
    del _L1_ffn_all

    return {
        "x": x,
        "cls_tok": cls_tok,
        "L0_tok_W": _L0_tok_in["W"],
        "L0_tok_b": _L0_tok_in["b"],
        "L0_attn_in_w": _L0_attn_in["in_w"],
        "L0_attn_conv_w": _L0_attn_in["conv_w"],
        "L0_attn_conv_b": _L0_attn_in["conv_b"],
        "L0_attn_A_log": _L0_attn_in["A_log"],
        "L0_attn_xd_w": _L0_attn_in["xd_w"],
        "L0_attn_xB_w": _L0_attn_in["xB_w"],
        "L0_attn_xC_w": _L0_attn_in["xC_w"],
        "L0_attn_dtp_w": _L0_attn_in["dtp_w"],
        "L0_attn_dtp_b": _L0_attn_in["dtp_b"],
        "L0_attn_D": _L0_attn_in["D"],
        "L0_attn_out_w": _L0_attn_in["out_w"],
        "L0_attn_ln_g": _L0_attn_in["ln_g"],
        "L0_attn_ln_b": _L0_attn_in["ln_b"],
        "L0_attn_merge_w": _L0_attn_in["merge_w"],
        "L0_ffn_sW1": _L0_ffn_in["sW1"],
        "L0_ffn_sb1": _L0_ffn_in["sb1"],
        "L0_ffn_sW2": _L0_ffn_in["sW2"],
        "L0_ffn_sb2": _L0_ffn_in["sb2"],
        "L0_ffn_sW3": _L0_ffn_in["sW3"],
        "L0_ffn_sb3": _L0_ffn_in["sb3"],
        "L0_ffn_eW1": _L0_ffn_in["eW1"],
        "L0_ffn_eb1": _L0_ffn_in["eb1"],
        "L0_ffn_eW2": _L0_ffn_in["eW2"],
        "L0_ffn_eb2": _L0_ffn_in["eb2"],
        "L0_ffn_eW3": _L0_ffn_in["eW3"],
        "L0_ffn_eb3": _L0_ffn_in["eb3"],
        "L0_ffn_gW": _L0_ffn_in["gW"],
        "L0_ffn_gb": _L0_ffn_in["gb"],
        "L1_attn_Wq": _L1_attn_in["Wq"],
        "L1_attn_Wk": _L1_attn_in["Wk"],
        "L1_attn_Wv": _L1_attn_in["Wv"],
        "L1_ffn_attention_mask": _L1_ffn_in["attention_mask"],
        "L1_ffn_wr": _L1_ffn_in["wr"],
        "L1_ffn_br": _L1_ffn_in["br"],
        "L1_ffn_w1": _L1_ffn_in["w1"],
        "L1_ffn_b1": _L1_ffn_in["b1"],
        "L1_ffn_w2": _L1_ffn_in["w2"],
        "L1_ffn_b2": _L1_ffn_in["b2"],
    }

def reference(x, cls_tok, L0_tok_W, L0_tok_b, L0_attn_in_w, L0_attn_conv_w, L0_attn_conv_b, L0_attn_A_log, L0_attn_xd_w, L0_attn_xB_w, L0_attn_xC_w, L0_attn_dtp_w, L0_attn_dtp_b, L0_attn_D, L0_attn_out_w, L0_attn_ln_g, L0_attn_ln_b, L0_attn_merge_w, L0_ffn_sW1, L0_ffn_sb1, L0_ffn_sW2, L0_ffn_sb2, L0_ffn_sW3, L0_ffn_sb3, L0_ffn_eW1, L0_ffn_eb1, L0_ffn_eW2, L0_ffn_eb2, L0_ffn_eW3, L0_ffn_eb3, L0_ffn_gW, L0_ffn_gb, L1_attn_Wq, L1_attn_Wk, L1_attn_Wv, L1_ffn_attention_mask, L1_ffn_wr, L1_ffn_br, L1_ffn_w1, L1_ffn_b1, L1_ffn_w2, L1_ffn_b2):
    import jax
    import jax.numpy as jnp
    def _L0_tok_ref(geom, W, b):
        import jax, jax.numpy as jnp
        import numpy as np
        HIDDEN_DIM = 512
        bias = jnp.einsum('bijf,hf->bijh', geom, W) + b
        return bias.mean(-1)

    def _L0_attn_ref(x, in_w, conv_w, conv_b, A_log, xd_w, xB_w, xC_w, dtp_w, dtp_b, D, out_w, ln_g, ln_b, merge_w):
        import jax, jax.numpy as jnp
        import numpy as np
        B_, S_, DM, DI, N_, R_, K_ = (2, 2048, 256, 512, 16, 32, 4)
        NB = 4

        def _layer_norm(x, g, b, eps=1e-05):
            m = jnp.mean(x, axis=-1, keepdims=True)
            v = jnp.mean(jnp.square(x - m), axis=-1, keepdims=True)
            return (x - m) * jax.lax.rsqrt(v + eps) * g + b

        def _ssm_scan(dA, dBx, C):

            def step(h, inp):
                dA_t, dBx_t, C_t = inp
                h = dA_t * h + dBx_t
                y = jnp.einsum('bdn,bn->bd', h, C_t)
                return (h, y)
            h0 = jnp.zeros(dA.shape[:1] + dA.shape[2:], dA.dtype)
            _, ys = jax.lax.scan(step, h0, (dA.transpose(1, 0, 2, 3), dBx.transpose(1, 0, 2, 3), C.transpose(1, 0, 2)))
            return ys.transpose(1, 0, 2)

        def _mamba_block(x, in_w, conv_w, conv_b, A_log, xd_w, xB_w, xC_w, dtp_w, dtp_b, D, out_w, g, b):
            res = x
            xn = _layer_norm(x, g, b)
            xz = xn @ in_w
            xs, z = jnp.split(xz, 2, axis=-1)
            xc = jax.lax.conv_general_dilated(xs.transpose(0, 2, 1), conv_w[:, None, :], (1,), [(K_ - 1, 0)], dimension_numbers=('NCH', 'OIH', 'NCH'), feature_group_count=DI)
            xc = jax.nn.silu((xc + conv_b[None, :, None]).transpose(0, 2, 1))
            delta = jax.nn.softplus(xc @ xd_w @ dtp_w + dtp_b)
            Bm = xc @ xB_w
            Cm = xc @ xC_w
            A = -jnp.exp(A_log)
            dA = jnp.exp(delta[..., None] * A)
            dBx = (delta * xc)[..., None] * Bm[:, :, None, :]
            y = _ssm_scan(dA, dBx, Cm) + D * xc
            return y * jax.nn.silu(z) @ out_w + res
        def blk(h, i):
            return _mamba_block(h, in_w[i], conv_w[i], conv_b[i], A_log[i], xd_w[i], xB_w[i], xC_w[i], dtp_w[i], dtp_b[i], D[i], out_w[i], ln_g[i], ln_b[i])
        fwd = blk(blk(x, 0), 1)
        bwd = blk(blk(x[:, ::-1], 2), 3)[:, ::-1]
        return jnp.concatenate([fwd, bwd], axis=-1) @ merge_w

    def _L0_ffn_ref(x, sW1, sb1, sW2, sb2, sW3, sb3, eW1, eb1, eW2, eb2, eW3, eb3, gW, gb):
        import jax, jax.numpy as jnp
        import numpy as np
        B, A = (4096, 8)
        IN, OUT = (256, 256)
        SH1, SH2 = (256, 128)
        EH1, EH2 = (128, 64)
        E, TOPK = (4, 2)

        def _shared_mlp(x, W1, b1, W2, b2, W3, b3):
            h = jax.nn.relu(x @ W1 + b1)
            h = jax.nn.relu(h @ W2 + b2)
            return h @ W3 + b3

        def _experts_mlp(x, eW1, eb1, eW2, eb2, eW3, eb3):
            h = jax.nn.relu(jnp.einsum('baf,efh->ebah', x, eW1) + eb1[:, None, None, :])
            h = jax.nn.relu(jnp.einsum('ebah,ehg->ebag', h, eW2) + eb2[:, None, None, :])
            o = jnp.einsum('ebag,ego->ebao', h, eW3) + eb3[:, None, None, :]
            return jnp.moveaxis(o, 0, -1)
        all_out = _experts_mlp(x, eW1, eb1, eW2, eb2, eW3, eb3)
        shared = _shared_mlp(x, sW1, sb1, sW2, sb2, sW3, sb3)
        gates = jax.nn.softmax(x @ gW + gb, axis=-1)
        topv, topi = jax.lax.top_k(gates, TOPK)
        topw = jax.nn.softmax(topv, axis=-1)
        sel = jnp.take_along_axis(all_out, topi[:, :, None, :], axis=-1)
        gated = jnp.sum(sel * topw[:, :, None, :], axis=-1)
        return shared + gated

    def _L1_attn_ref(x, Wq, Wk, Wv):
        import jax, jax.numpy as jnp
        import numpy as np
        B, N, D = (8, 2048, 256)
        q = jnp.einsum('bnd,ed->bne', x, Wq)
        k = jnp.einsum('bnd,ed->bne', x, Wk)
        v = jnp.einsum('bnd,ed->bne', x, Wv)
        energy = jnp.einsum('bqd,bkd->bqk', q, k)
        scaling = jnp.asarray(x.shape[-1] ** (-0.5), x.dtype)
        att = jax.nn.softmax(energy, axis=-1) * scaling
        out = jnp.einsum('bqk,bkv->bqv', att, v)
        return out

    def _L1_ffn_ref(x, attention_mask, wr, br, w1, b1, w2, b2):
        import jax, jax.numpy as jnp
        import numpy as np
        B, S, D = (8, 4096, 256)
        H = 4 * D
        CAPACITY = 0.5
        b, s, d = x.shape
        weights = (jnp.einsum('bsd,do->bso', x, wr) + br)[..., 0]
        k = max(1, int(CAPACITY * s))
        kk = k - 1 if k > 1 else 1
        _, idx = jax.lax.top_k(weights, k)
        sel_idx = idx[:, :kk]
        sel = jnp.take_along_axis(x, sel_idx[:, :, None], axis=1)
        h = jax.nn.gelu(jnp.einsum('bkd,dh->bkh', sel, w1) + b1)
        y = jnp.einsum('bkh,hd->bkd', h, w2) + b2
        w_sel = jnp.take_along_axis(weights, sel_idx, axis=1)
        y = y * w_sel[..., None]
        batch_idx = jnp.arange(b)[:, None]
        processed = jnp.zeros_like(x).at[batch_idx, sel_idx].set(y)
        return processed + x

    h = _L0_tok_ref(x, L0_tok_W, L0_tok_b)
    h = jnp.concatenate([jnp.broadcast_to(cls_tok, (h.shape[0], 1, h.shape[2])), h], axis=1)
    h = h + _L0_attn_ref(_layernorm(h, axis=-1), L0_attn_in_w, L0_attn_conv_w, L0_attn_conv_b, L0_attn_A_log, L0_attn_xd_w, L0_attn_xB_w, L0_attn_xC_w, L0_attn_dtp_w, L0_attn_dtp_b, L0_attn_D, L0_attn_out_w, L0_attn_ln_g, L0_attn_ln_b, L0_attn_merge_w)
    h = h + _L0_ffn_ref(_layernorm(h, axis=-1), L0_ffn_sW1, L0_ffn_sb1, L0_ffn_sW2, L0_ffn_sb2, L0_ffn_sW3, L0_ffn_sb3, L0_ffn_eW1, L0_ffn_eb1, L0_ffn_eW2, L0_ffn_eb2, L0_ffn_eW3, L0_ffn_eb3, L0_ffn_gW, L0_ffn_gb)
    h = h + _L1_attn_ref(_layernorm(h, axis=-1), L1_attn_Wq, L1_attn_Wk, L1_attn_Wv)
    h = h + _L1_ffn_ref(_layernorm(h, axis=-1), L1_ffn_attention_mask, L1_ffn_wr, L1_ffn_br, L1_ffn_w1, L1_ffn_b1, L1_ffn_w2, L1_ffn_b2)
    return h


_drawn_inputs = setup_inputs


def setup_inputs(seed=0):
    import zlib

    import numpy as np

    out = dict(_drawn_inputs(seed))
    spreads = {'L0_attn_conv_b': (0.0, 0.614),
     'L0_attn_D': (1.0, 0.6),
     'L0_attn_ln_g': (1.0, 0.6),
     'L0_attn_ln_b': (0.0, 0.8),
     'L0_ffn_sb1': (0.0, 0.8),
     'L0_ffn_sb2': (0.0, 0.548),
     'L0_ffn_sb3': (0.0, 0.288),
     'L0_ffn_eb1': (0.0, 2.0),
     'L0_ffn_eb2': (0.0, 0.8),
     'L0_ffn_eb3': (0.0, 0.397),
     'L0_ffn_gb': (0.0, 0.8),
     'L1_ffn_b1': (0.0, 0.8),
     'L1_ffn_b2': (0.0, 0.701)}
    factors = {'L0_tok_b': 64.0,
     'L0_attn_conv_w': 2.866,
     'L0_attn_A_log': 8.0,
     'L0_attn_xd_w': 8.0,
     'L0_attn_xB_w': 8.0,
     'L0_attn_xC_w': 8.0,
     'L0_attn_dtp_w': 8.0,
     'L0_attn_dtp_b': 8.0,
     'L1_ffn_wr': 2.868,
     'L1_ffn_w1': 4.923,
     'L1_ffn_w2': 4.576,
     'L0_ffn_eW1': 3.725,
     'L0_ffn_eW2': 3.048,
     'L0_ffn_gW': 2.747,
     'L1_attn_Wq': 3.16,
     'L1_attn_Wk': 3.179,
     'L1_attn_Wv': 3.238}
    for name, (base, spread) in spreads.items():
        noise = np.random.default_rng([zlib.crc32(name.encode()), seed]).standard_normal(out[name].shape)
        drawn = base * np.exp(spread * noise) if base else spread * noise
        out[name] = jnp.asarray(drawn.astype(out[name].dtype))
    for name, factor in factors.items():
        out[name] = (out[name] * factor).astype(out[name].dtype)
    return out
```

```python
import concourse.bass as bass
from concourse import mybir
from contextlib import ExitStack

F32 = mybir.dt.float32
ALU = mybir.AluOpType
ACT = mybir.ActivationFunctionType
AX = mybir.AxisListType

P = 128
NBATCH, S, DM = 32, 257, 256
BANK = 512
NB = 2
T = NB * S
GROUPS = NBATCH // NB
CM = DM // P
DI, NST, RNK, KW = 512, 16, 32, 4
CI = DI // P
NU = 2
PAIRS = NST // NU
UNITS = CI * PAIRS
NHB, NDA = 4, 2
BLOCK_OF_JOB = (0, 2, 1, 3)
EPS = 1e-5
LN_SLACK = 2.0 ** -23


def mamba_phase(nc, a, h_mid, bc_dram):

    prepare = ["mean", "var", "xs0", "xs1", "cv0", "xs2", "cv1", "xs3", "cv2", "cv3", "xp", "dt0", "dt1", "dt2", "dt3"]
    slots = {}
    for name in ["t0", "t1", "tmean", "tvar"] + prepare:
        slots[name, 0] = len(slots)
    for name in ["z0", "z1", "z2", "z3"]:
        slots[name, 0] = len(slots)
    for name in prepare:
        slots[name, 1] = len(slots)
    n_first = len(slots)
    for jj in (1, 2, 3, 4):
        for name in ["o0", "o1"]:
            slots[name, jj - 1] = len(slots)
        if jj == 4:
            for name in ["m0", "m1"]:
                slots[name, 3] = len(slots)
        if jj == 3:
            for name in ["t0", "t1", "tmean", "tvar"]:
                slots[name, 4] = len(slots)
        for name in ["z0", "z1", "z2", "z3"]:
            slots[name, jj] = len(slots)
        for name in prepare:
            slots[name, jj + 1] = len(slots)
    n_body = len(slots) - n_first
    assert n_first % 2 == 0 and n_body % 2 == 0

    final_slots = {}
    for key in [("z0", 3), ("z1", 3), ("z2", 3), ("z3", 3), ("o0", 3), ("o1", 3), ("m0", 3), ("m1", 3)]:
        final_slots[key] = slots["o1", 2] + 1 + len(final_slots)

    def slot(name, g, jj):
        if isinstance(g, int) and g == GROUPS - 1 and (name, jj) in final_slots:
            return final_slots[name, jj]
        return slots[name, jj]

    norms = {("tok", 0): 0, ("job", 0): 1, ("job", 1): 2}
    for key in [("job", 2), ("job", 3), ("tok", 4), ("job", 4), ("job", 5)]:
        norms[key] = len(norms)

    def job_count(g, jj, per_job, k):
        return g * (4 * per_job) + (jj * per_job + k)

    def nth(name, g, jj):
        return g * (n_body // 2) + (slot(name, g, jj) // 2 + 1)

    def positive(count):
        return not isinstance(count, int) or count > 0

    registers = {}

    def in_registers(eng, *values):
        held = []
        for i, value in enumerate(values):
            if not isinstance(value, int):
                register = registers.get((eng.engine, i)) or eng.alloc_register(f"wait_value{i}")
                registers[eng.engine, i] = register
                eng.reg_mov(register, value)
                value = register
            held.append(value)
        return held

    with ExitStack() as ctx:
        def sb(name, shape):
            return ctx.enter_context(nc.sbuf_tensor(name, shape, F32))

        def sem(name):
            return ctx.enter_context(nc.semaphore(name))

        ident = sb("ident", [P, P])
        tok_ident = sb("tok_ident", [P, 4, P])
        mean_w = sb("mean_w", [P, P])
        tok_mean = sb("tok_mean", [P, P])
        tok_w = sb("tok_w", [P, CI, 5])
        tok_wb = sb("tok_wb", [P, 5])
        eps_t = sb("eps_t", [P, 1])
        sq_bias = sb("sq_bias", [P, 1])
        neg_a = sb("neg_a", [P, 4, CI, NST])
        conv_w = sb("conv_w", [P, 4, CI, KW])
        conv_b = sb("conv_b", [P, 4, CI])
        dtp_b = sb("dtp_b", [P, 4, CI])
        d_skip = sb("d_skip", [P, 4, CI])
        ln_g = sb("ln_g", [P, 4, CM])
        ln_b = sb("ln_b", [P, 4, CM])
        merge_w = sb("merge_w", [P, 2 * CM, DM])
        in_w = sb("in_w", [P, CM, 2 * DI])
        out_w = sb("out_w", [P, CI, DM])
        xp_w = sb("xp_w", [P, CI, RNK + 2 * NST])
        dt_w = sb("dt_w", [RNK, DI])
        x_in = sb("x_in", [P, 2, P, 4])
        h_next = sb("h_next", [P, CM, NB, S])
        h_cur = sb("h_cur", [P, CM, NB, S])
        x_f = sb("x_f", [P, CM, NB, S])
        x_b = sb("x_b", [P, CM, NB, S])
        o_f = sb("o_f", [P, CM, NB, S])
        cen = sb("cen", [P, CM, NB, S])
        sq = sb("sq", [P, CM, NB, S])
        rstd = sb("rstd", [P, NB, S])
        xn = sb("xn", [P, CM, NB, S])
        xs_pad = sb("xs_pad", [P, 2, NB, KW - 1 + S])
        conv_diag = sb("conv_diag", [P, 2, KW, P])
        xc = sb("xc", [P, 2, CI, NB, S])
        dtbc = sb("dtbc", [RNK + 2 * NST, NB, S])
        sp_e = sb("sp_e", [P, NB, S])
        sp_q = sb("sp_q", [P, NB, S])
        sp_l = sb("sp_l", [P, NB, S])
        sp_r = sb("sp_r", [P, NB, S])
        delta = sb("delta", [P, CI, NB, S])
        u_buf = sb("u_buf", [P, 2, NB, S])
        decay = sb("decay", [P, NDA, NU, NB, S])
        hb = sb("hb", [P, NHB, NU, NB, S])
        b_all = sb("b_all", [P, PAIRS, NU, NB, S])
        c_all = sb("c_all", [P, PAIRS, NU, NB, S])
        sz = sb("sz", [P, CI, NB, S])
        y_skip = sb("y_skip", [P, NB, S])

        y_ps = [ctx.enter_context(nc.psum_tensor(f"y_ps{i}", [P, NB, BANK], F32)) for i in range(2)]
        w_ps = [ctx.enter_context(nc.psum_tensor(f"w_ps{i}", [P, NB, BANK], F32)) for i in range(2)]

        consts_loaded = sem("consts_loaded")
        zeros_set = sem("zeros_set")
        ident_set = sem("ident_set")
        setup_pe = sem("setup_pe")
        setup_act = sem("setup_act")
        in_w_loaded = sem("in_w_loaded")
        out_w_loaded = sem("out_w_loaded")
        x_loaded = [sem(f"x_loaded{i}") for i in range(2)]
        x_used = sem("x_used")
        work_full = [sem(f"work_full{i}") for i in range(2)]
        work_read = [sem(f"work_read{i}") for i in range(2)]
        h_cur_copied = sem("h_cur_copied")
        x0_ready = sem("x0_ready")
        x_b_copied = sem("x_b_copied")
        squared = sem("squared")
        rstd_ready = sem("rstd_ready")
        xhat_ready = sem("xhat_ready")
        xn_ready = sem("xn_ready")
        diag_ready = sem("diag_ready")
        bc_stored = sem("bc_stored")
        bc_loaded = [sem(f"bc_loaded{i}") for i in range(PAIRS)]
        sp_abs = sem("sp_abs")
        sp_exp = sem("sp_exp")
        sp_logs = sem("sp_logs")
        sp_sums = sem("sp_sums")
        delta_ready = sem("delta_ready")
        u_ready = sem("u_ready")
        decays_ready = sem("decays_ready")
        b_done = sem("b_done")
        scan_done = sem("scan_done")
        c_done = [sem("c_done_vector"), sem("c_done_pool")]
        y_added = sem("y_added")
        y_read = sem("y_read")
        yz_ready = sem("yz_ready")
        h_mid_stored = sem("h_mid_stored")

        n_const_dmas = CI + 1 + 1 + NB * CM + 4 * 7

        def on(jj, u):
            return jj + u // UNITS, u % UNITS

        def banks(name, g, jj):
            return w_ps[slot(name, g, jj) % 2]

        def full_of(name, g, jj):
            return work_full[slot(name, g, jj) % 2]

        def read_of(name, g, jj):
            return work_read[slot(name, g, jj) % 2]

        def stream(jj):
            return x_b if jj % 2 else x_f

        def run(eng, lead_in, period, tail):
            lead_in()
            period(0, 0, True, False)
            with eng.Fori(0, GROUPS - 1) as g:
                for jj in (1, 2, 3, 4):
                    period(g, jj, False, False)
            for jj in (1, 2, 3):
                period(GROUPS - 1, jj, False, jj == 3)
            tail(GROUPS - 1)

        block = ctx.enter_context(nc.Block())

        @block.sync
        def _(sp):
            def const(dst, src):
                sp.dma_start(dst, src, allow_slow_non_contiguous=True).then_inc(consts_loaded, 16)

            def load_weights(jj):
                k = BLOCK_OF_JOB[jj % 4]
                sp.dma_start(in_w[:, :, :], a["L0_attn_in_w"][k].rearrange("(c p) n -> p c n", p=P)).then_inc(in_w_loaded, 16)
                for name, lo, hi in (("xd_w", 0, RNK), ("xB_w", RNK, RNK + NST), ("xC_w", RNK + NST, RNK + 2 * NST)):
                    sp.dma_start(xp_w[:, :, lo:hi], a[f"L0_attn_{name}"][k].rearrange("(c p) n -> p c n", p=P),
                                 allow_slow_non_contiguous=True).then_inc(in_w_loaded, 16)
                sp.dma_start(dt_w[:, :], a["L0_attn_dtp_w"][k]).then_inc(in_w_loaded, 16)

            def load_out_w(jj):
                sp.dma_start(out_w[:, :, :], a["L0_attn_out_w"][BLOCK_OF_JOB[jj % 4]].rearrange("(c p) n -> p c n", p=P)
                             ).then_inc(out_w_loaded, 16)

            def load_x(g, jj):
                for n in range(8):
                    c, b, half = n // 4, n // 2 % 2, n % 2
                    if positive(g * 8 + 8 * (jj // 4) + n - 1):
                        sp.wait_ge(x_used, g * 8 + 8 * (jj // 4) + n - 1)
                    src = a["x"][bass.ds(g * NB + (jj // 4 * NB + b), 1), half * P:(half + 1) * P, c * P:(c + 1) * P, :]
                    sp.dma_start(x_in[:, n % 2, :, :], src.rearrange("o i j f -> (o i) j f")).then_inc(x_loaded[n % 2], 16)

            def bring_bc(g, jj):
                sp.wait_ge(read_of("xp", g, jj), nth("xp", g, jj))
                rows = bc_dram[jj % 2]
                sp.dma_start(rows, dtbc[RNK:, :, :].rearrange("r b s -> r (b s)")).then_inc(bc_stored, 16)
                for n in range(PAIRS):
                    counts = in_registers(sp, job_count(g, jj, 16, 16), job_count(g, jj - 1, UNITS, 3 * PAIRS + n + 1),
                                          job_count(g, jj - 1, UNITS // 2, (3 * PAIRS + n) // 2 + 1))
                    if n == 0:
                        sp.wait_ge(bc_stored, counts[0])
                    if positive(counts[1]):
                        sp.wait_ge(b_done, counts[1])
                        sp.wait_ge(c_done[n % 2], counts[2])
                    for dst, first_row in ((b_all, 0), (c_all, NST)):
                        r = first_row + NU * n
                        sp.dma_start(dst[:, n, :, :, :].rearrange("p n b s -> p (n b s)"),
                                     rows[r:r + NU, :].rearrange("r t -> (r t)").partition_broadcast(P)
                                     ).then_inc(bc_loaded[n], 16)

            def store_h(g):
                sp.wait_ge(read_of("m1", g, 3), nth("m1", g, 3))
                for c in range(CM):
                    sp.dma_start(h_mid[c, :, bass.ds(g * NB, NB), :], h_cur[:, c, :, :]).then_inc(h_mid_stored, 16)

            def lead_in():
                for c in range(CI):
                    const(tok_w[:, c, 0:4], a["L0_tok_W"][c * P:(c + 1) * P, :])
                const(tok_w[:, :, 4:5], a["L0_tok_b"].rearrange("(c p o) -> p c o", p=P, o=1))
                const(merge_w[:, :, :], a["L0_attn_merge_w"].rearrange("(c p) n -> p c n", p=P))
                cls = a["cls_tok"].rearrange("a b (c p) -> p c (a b)", p=P)
                for b in range(NB):
                    for c in range(CM):
                        const(h_next[:, c, b, 0:1], cls[:, c, :])
                for k in range(4):
                    const(neg_a[:, k, :, :], a["L0_attn_A_log"][k].rearrange("(c p) n -> p c n", p=P))
                    const(conv_w[:, k, :, :], a["L0_attn_conv_w"][k].rearrange("(c p) n -> p c n", p=P))
                    for dst, name in ((conv_b, "conv_b"), (dtp_b, "dtp_b"), (d_skip, "D"), (ln_g, "ln_g"), (ln_b, "ln_b")):
                        const(dst[:, k, :], a[f"L0_attn_{name}"][k].rearrange("(c p) -> p c", p=P))
                load_weights(0)
                load_x(0, 0)
                bring_bc(0, 0)

            def period(g, jj, first, last):
                if jj == 4:
                    store_h(g)
                if jj == 3 and not last:
                    load_x(g, 4)
                if not first:
                    sp.wait_ge(full_of("o1", g, jj - 1), nth("o1", g, jj - 1))
                load_out_w(jj)
                if not last:
                    sp.wait_ge(full_of("z3", g, jj), nth("z3", g, jj))
                    load_weights(jj + 1)
                    bring_bc(g, jj + 1)

            def tail(g):
                store_h(g)
                sp.wait_ge(h_mid_stored, GROUPS * CM * 16)

            run(sp, lead_in, period, tail)

        @block.gpsimd
        def _(pool):
            pool.memset(xs_pad[:, :, :, :], 0.0).then_inc(zeros_set, 1)
            pool.memset(decay[:, :, :, :, :], 0.0).then_inc(zeros_set, 1)
            pool.memset(mean_w[:, :], 1.0 / DM).then_inc(zeros_set, 1)
            pool.memset(tok_mean[:, :], 1.0 / DI).then_inc(zeros_set, 1)
            pool.memset(eps_t[:, :], EPS).then_inc(zeros_set, 1)
            pool.memset(sq_bias[:, :], -0.75 * 3 ** -0.5).then_inc(zeros_set, 1)
            pool.memset(ident[:, :], 0.0).then_inc(ident_set, 1)
            pool.wait_ge(ident_set, 1)
            pool.affine_select(out=ident[:, :], in_=ident[:, :], compare_op=ALU.not_equal, fill=1.0, base=0,
                               pattern=[[-1, P]], channel_multiplier=1).then_inc(ident_set, 1)

            def b_times_u(g, jj, u):
                jj, u = on(jj, u)
                c, n = u // PAIRS, u % PAIRS
                counts = in_registers(pool, job_count(g, jj, 32, 32), job_count(g, jj, CI, c + 1),
                                      job_count(g, jj, UNITS, u + 1 - NHB))
                if c == 0:
                    pool.wait_ge(bc_loaded[n], counts[0])
                if n == 0:
                    pool.wait_ge(u_ready, counts[1])
                if positive(counts[2]):
                    pool.wait_ge(y_added, counts[2])
                pool.tensor_tensor(hb[:, u % NHB, :, :, :].rearrange("p n b s -> p n (b s)"),
                                   b_all[:, n, :, :, :].rearrange("p n b s -> p n (b s)"),
                                   u_buf[:, c % 2, :, :].rearrange("p b s -> p (b s)").unsqueeze(1).to_broadcast([P, NU, T]),
                                   ALU.mult).then_inc(b_done, 1)

            def c_times_h(g, jj, u):
                jj, u = on(jj, u)
                if u % 2 == 0:
                    return
                pool.wait_ge(scan_done, job_count(g, jj, UNITS, u + 1))
                h = hb[:, u % NHB, :, :, :].rearrange("p n b s -> p (n b s)")
                pool.tensor_tensor(h, h, c_all[:, u % PAIRS, :, :, :].rearrange("p n b s -> p (n b s)"),
                                   ALU.mult).then_inc(c_done[1], 1)

            def lead_in():
                b_times_u(0, 0, 0)

            def period(g, jj, first, last):
                for u in range(UNITS):
                    if not (last and u == UNITS - 1):
                        b_times_u(g, jj, u + 1)
                    if not (first and u == 0):
                        c_times_h(g, jj, u - 1)

            def tail(g):
                c_times_h(g, 3, UNITS - 1)

            run(pool, lead_in, period, tail)

        @block.scalar
        def _(act):
            func = nc.scalar.activation

            def tokens(g, jj, c):
                act.wait_ge(full_of(f"t{c}", g, jj), nth(f"t{c}", g, jj))
                w = banks(f"t{c}", g, jj)
                func(h_next[:, c, :, 1:S], w[:, :, 1:S], ACT.Identity, bias=tok_wb[:, 4:5]).then_inc(read_of(f"t{c}", g, jj), 1)

            def copy_h(g, jj):
                act.wait_ge(read_of("t1", g, jj), nth("t1", g, jj))
                if positive((g + jj // 4) * (16 * CM)):
                    act.wait_ge(h_mid_stored, (g + jj // 4) * (16 * CM))
                func(h_cur[:, :, :, :], h_next[:, :, :, :], ACT.Identity).then_inc(h_cur_copied, 1)

            def square(kind, g, jj):
                act.wait_ge(read_of("tmean" if kind == "tok" else "mean", g, jj), nth("tmean" if kind == "tok" else "mean", g, jj))
                for c in range(CM):
                    last = func(sq[:, c, :, :], cen[:, c, :, :], ACT.Square)
                last.then_inc(squared, 1)

            def inverse_deviation(kind, g, jj):
                name = "tvar" if kind == "tok" else "var"
                act.wait_ge(full_of(name, g, jj), nth(name, g, jj))
                w = banks(name, g, jj)
                func(rstd[:, :, :], w[:, :, 0:S], ACT.Ln, bias=eps_t[:, 0:1]).then_inc(read_of(name, g, jj), 1)
                act.wait_ge(read_of(name, g, jj), nth(name, g, jj))
                func(rstd[:, :, :], rstd[:, :, :], ACT.Exp, scale=-0.5).then_inc(rstd_ready, 1)

            def gain_and_bias(g, jj):
                k = BLOCK_OF_JOB[jj % 4]
                act.wait_ge(xhat_ready, job_count(g, jj, 1, 1))
                for c in range(CM):
                    last = func(xn[:, c, :, :], cen[:, c, :, :], ACT.Identity, scale=ln_g[:, k, c:c + 1],
                                bias=ln_b[:, k, c:c + 1])
                last.then_inc(xn_ready, 1)

            def start_backward(g, jj):
                act.wait_ge(x0_ready, g + jj // 4 + 1)
                if jj > 1:
                    act.wait_ge(full_of("m1", g, jj - 2), nth("m1", g, jj - 2))
                for c in range(CM):
                    last = func(x_b[:, c, :, :], x_f[:, c, :, ::-1], ACT.Identity)
                last.then_inc(x_b_copied, 1)

            def conv_input(g, jj, c):
                k = BLOCK_OF_JOB[jj % 4]
                act.wait_ge(full_of(f"xs{c}", g, jj), nth(f"xs{c}", g, jj))
                w = banks(f"xs{c}", g, jj)
                func(xs_pad[:, c % 2, :, KW - 1:], w[:, :, 0:S], ACT.Identity).then_inc(read_of(f"xs{c}", g, jj), 1)
                for tap in range(KW):
                    last = func(conv_diag[:, c % 2, tap, :], ident[:, :], ACT.Identity, scale=conv_w[:, k, c, tap:tap + 1])
                last.then_inc(diag_ready, 1)

            def conv_output(g, jj, c):
                k = BLOCK_OF_JOB[jj % 4]
                act.wait_ge(full_of(f"cv{c}", g, jj), nth(f"cv{c}", g, jj))
                w = banks(f"cv{c}", g, jj)
                if c == 0:
                    if positive(job_count(g, jj - 2, CI, CI)):
                        act.wait_ge(yz_ready, job_count(g, jj - 2, CI, CI))
                func(xc[:, jj % 2, c, :, :], w[:, :, 0:S], ACT.Silu, bias=conv_b[:, k, c:c + 1]).then_inc(read_of(f"cv{c}", g, jj), 1)

            def projections(g, jj):
                act.wait_ge(full_of("xp", g, jj), nth("xp", g, jj))
                w = banks("xp", g, jj)
                if positive(job_count(g, jj - 1, 16, 16)):
                    act.wait_ge(bc_stored, job_count(g, jj - 1, 16, 16))
                func(dtbc[:, :, :], w[0:RNK + 2 * NST, :, 0:S], ACT.Identity).then_inc(read_of("xp", g, jj), 1)

            def softplus(g, jj, c):
                k = BLOCK_OF_JOB[jj % 4]
                act.wait_ge(full_of(f"dt{c}", g, jj), nth(f"dt{c}", g, jj))
                w = banks(f"dt{c}", g, jj)
                if positive(job_count(g, jj, CI, c)):
                    act.wait_ge(delta_ready, job_count(g, jj, CI, c))
                func(sp_e[:, :, :], w[:, :, 0:S], ACT.Abs, bias=dtp_b[:, k, c:c + 1]).then_inc(sp_abs, 1)
                func(sp_r[:, :, :], w[:, :, 0:S], ACT.Relu, bias=dtp_b[:, k, c:c + 1]).then_inc(read_of(f"dt{c}", g, jj), 1)
                act.wait_ge(sp_abs, job_count(g, jj, CI, c + 1))
                func(sp_e[:, :, :], sp_e[:, :, :], ACT.Exp, scale=-1.0).then_inc(sp_exp, 1)
                act.wait_ge(sp_exp, job_count(g, jj, CI, c + 1))
                func(sp_q[:, :, :], sp_e[:, :, :], ACT.Square, scale=3 ** -0.5, bias=sq_bias[:, 0:1])
                func(sp_l[:, :, :], sp_e[:, :, :], ACT.Ln, bias=1.0).then_inc(sp_logs, 1)

            def gate(g, jj, c):
                act.wait_ge(full_of(f"z{c}", g, jj), nth(f"z{c}", g, jj))
                w = banks(f"z{c}", g, jj)
                func(sz[:, c, :, :], w[:, :, 0:S], ACT.Silu).then_inc(read_of(f"z{c}", g, jj), 1)

            def decays(g, jj, u):
                jj, u = on(jj, u)
                c, n = u // PAIRS, u % PAIRS
                k = BLOCK_OF_JOB[jj % 4]
                if n == 0:
                    act.wait_ge(delta_ready, job_count(g, jj, CI, c + 1))
                if positive(job_count(g, jj, UNITS, u + 1 - NDA)):
                    act.wait_ge(scan_done, job_count(g, jj, UNITS, u + 1 - NDA))
                for i in range(NU):
                    last = func(decay[:, u % NDA, i, :, 1:S], delta[:, c, :, 1:S], ACT.Exp,
                                scale=neg_a[:, k, c, NU * n + i:NU * n + i + 1])
                last.then_inc(decays_ready, 1)

            def lead_in():
                act.wait_ge(consts_loaded, 16 * n_const_dmas)
                act.wait_ge(zeros_set, 6)
                act.wait_ge(ident_set, 2)
                func(neg_a[:, :, :, :], neg_a[:, :, :, :], ACT.Exp).then_inc(setup_act, 1)
                act.wait_ge(setup_pe, 1)
                func(tok_wb[:, :], w_ps[1][:, 0, 0:5], ACT.Identity).then_inc(setup_act, 1)
                act.wait_ge(setup_act, 2)
                func(neg_a[:, :, :, :], neg_a[:, :, :, :], ACT.Identity, scale=-1.0).then_inc(setup_act, 1)
                for f in range(4):
                    func(tok_ident[:, f, :], ident[:, :], ACT.Identity, scale=tok_wb[:, f:f + 1]).then_inc(setup_act, 1)
                tokens(0, 0, 0)
                tokens(0, 0, 1)
                copy_h(0, 0)
                square("tok", 0, 0)
                inverse_deviation("tok", 0, 0)
                prepare_front(0, 0)
                prepare_back(0, 0)
                for c in range(CI):
                    softplus(0, 0, c)
                act.wait_ge(setup_act, 7)
                decays(0, 0, 0)

            def prepare_front(g, jj):
                square("job", g, jj)
                inverse_deviation("job", g, jj)
                gain_and_bias(g, jj)

            def prepare_back(g, jj):
                conv_input(g, jj, 0)
                conv_input(g, jj, 1)
                conv_output(g, jj, 0)
                conv_input(g, jj, 2)
                conv_output(g, jj, 1)
                conv_input(g, jj, 3)
                conv_output(g, jj, 2)
                conv_output(g, jj, 3)
                projections(g, jj)

            def period(g, jj, first, last):
                for u in range(UNITS):
                    if not (last and u == UNITS - 1):
                        decays(g, jj, u + 1)
                    if jj == 3 and not last:
                        if u == 5:
                            tokens(g, 4, 0)
                            tokens(g, 4, 1)
                        if u == 6:
                            square("tok", g, 4)
                        if u == 8:
                            inverse_deviation("tok", g, 4)
                    if jj == 4 and u == 7:
                        copy_h(g, 4)
                    if jj in (0, 4) and u == 6:
                        start_backward(g, jj + 1)
                    if u == 4 + 3 * (jj == 4) + 5 * (jj == 3):
                        for c in range(CI):
                            gate(g, jj, c)
                    if last:
                        continue
                    if u == 11:
                        square("job", g, jj + 1)
                    if u == 12:
                        inverse_deviation("job", g, jj + 1)
                    if u == 13:
                        gain_and_bias(g, jj + 1)
                    if u == 15:
                        conv_input(g, jj + 1, 0)
                        conv_input(g, jj + 1, 1)
                    if u == 16:
                        conv_output(g, jj + 1, 0)
                        conv_input(g, jj + 1, 2)
                    if u == 17:
                        conv_output(g, jj + 1, 1)
                        conv_input(g, jj + 1, 3)
                    if u == 19:
                        conv_output(g, jj + 1, 2)
                        conv_output(g, jj + 1, 3)
                    if u == 21:
                        projections(g, jj + 1)
                    if u in (25, 27, 29, 31):
                        if u == 31:
                            continue
                        softplus(g, jj + 1, (u - 25) // 2)
                if not last:
                    softplus(g, jj + 1, 3)

            def tail(g):
                pass

            run(act, lead_in, period, tail)

        @block.vector
        def _(dve):
            def centre(kind, g, jj):
                name = "tmean" if kind == "tok" else "mean"
                x = h_next if kind == "tok" else stream(jj)
                dve.wait_ge(full_of(name, g, jj), nth(name, g, jj))
                w = banks(name, g, jj)
                for c in range(CM):
                    last = dve.tensor_tensor(cen[:, c, :, :], x[:, c, :, :], w[:, :, 0:S], ALU.subtract)
                last.then_inc(read_of(name, g, jj), 1)

            def normalize(kind, g, jj):
                i = norms[kind, jj]
                dve.wait_ge(rstd_ready, g * 5 + i + 1)
                if kind == "tok" and jj:
                    dve.wait_ge(full_of("tvar", g, jj), nth("tvar", g, jj))
                dst = x_f if kind == "tok" else cen
                for c in range(CM):
                    last = dve.tensor_tensor(dst[:, c, :, :], cen[:, c, :, :], rstd[:, :, :], ALU.mult)
                last.then_inc(x0_ready if kind == "tok" else xhat_ready, 1)

            def step_size(g, jj, c):
                dve.wait_ge(sp_logs, job_count(g, jj, CI, c + 1))
                dve.scalar_tensor_tensor(out=sp_q[:, :, :], in0=sp_q[:, :, :], scalar=13 / 16, in1=sp_e[:, :, :],
                                         op0=ALU.add, op1=ALU.mult).then_inc(sp_sums, 1)
                dve.wait_ge(sp_sums, job_count(g, jj, 2 * CI, 2 * c + 1))
                dve.scalar_tensor_tensor(out=sp_l[:, :, :], in0=sp_l[:, :, :], scalar=LN_SLACK, in1=sp_q[:, :, :],
                                         op0=ALU.add, op1=ALU.min).then_inc(sp_sums, 1)
                dve.wait_ge(sp_sums, job_count(g, jj, 2 * CI, 2 * c + 2))
                if positive(job_count(g, jj - 1, UNITS, PAIRS * (c + 1))):
                    dve.wait_ge(decays_ready, job_count(g, jj - 1, UNITS, PAIRS * (c + 1)))
                dve.tensor_tensor(delta[:, c, :, :], sp_l[:, :, :], sp_r[:, :, :], ALU.add).then_inc(delta_ready, 1)

            def delta_x(g, jj, c):
                dve.wait_ge(delta_ready, job_count(g, jj, CI, c + 1))
                if c == 0:
                    dve.wait_ge(read_of("cv3", g, jj), nth("cv3", g, jj))
                if positive(job_count(g, jj, UNITS, PAIRS * (c - 1))):
                    dve.wait_ge(b_done, job_count(g, jj, UNITS, PAIRS * (c - 1)))
                dve.tensor_tensor(u_buf[:, c % 2, :, :], delta[:, c, :, :], xc[:, jj % 2, c, :, :], ALU.mult).then_inc(u_ready, 1)

            def scan(g, jj, u):
                jj, u = on(jj, u)
                dve.wait_ge(decays_ready, job_count(g, jj, UNITS, u + 1))
                dve.wait_ge(b_done, job_count(g, jj, UNITS, u + 1))
                h = hb[:, u % NHB, :, :, :].rearrange("p n b s -> p (n b s)")
                dve.tensor_tensor_scan(h, decay[:, u % NDA, :, :, :].rearrange("p n b s -> p (n b s)"), h, 0.0,
                                       ALU.mult, ALU.add).then_inc(scan_done, 1)

            def c_times_h(g, jj, u):
                jj, u = on(jj, u)
                if u % 2:
                    return
                dve.wait_ge(scan_done, job_count(g, jj, UNITS, u + 1))
                dve.wait_ge(bc_loaded[u % PAIRS], job_count(g, jj, 32, 32))
                h = hb[:, u % NHB, :, :, :].rearrange("p n b s -> p (n b s)")
                dve.tensor_tensor(h, h, c_all[:, u % PAIRS, :, :, :].rearrange("p n b s -> p (n b s)"),
                                  ALU.mult).then_inc(c_done[0], 1)

            def output(g, jj, c):
                k = BLOCK_OF_JOB[jj % 4]
                dve.wait_ge(y_added, job_count(g, jj, UNITS, PAIRS * (c + 1)))
                dve.scalar_tensor_tensor(out=y_skip[:, :, :], in0=xc[:, jj % 2, c, :, :], scalar=d_skip[:, k, c:c + 1],
                                         in1=y_ps[c % 2][:, :, 0:S], op0=ALU.mult, op1=ALU.add).then_inc(y_read, 1)
                dve.wait_ge(y_read, job_count(g, jj, CI, c + 1))
                dve.wait_ge(read_of(f"z{c}", g, jj), nth(f"z{c}", g, jj))
                dve.tensor_tensor(sz[:, c, :, :], y_skip[:, :, :], sz[:, c, :, :], ALU.mult).then_inc(yz_ready, 1)

            def residual(g, jj, c):
                name = f"o{c}"
                dve.wait_ge(full_of(name, g, jj), nth(name, g, jj))
                w = banks(name, g, jj)
                if jj % 4 == 0:
                    dve.wait_ge(x_b_copied, g + jj // 4 + 1)
                x = stream(jj)
                dst = o_f if jj % 4 == 2 else x
                dve.tensor_tensor(dst[:, c, :, :], x[:, c, :, :], w[:, :, 0:S], ALU.add).then_inc(read_of(name, g, jj), 1)

            def merged(g, c):
                dve.wait_ge(full_of(f"m{c}", g, 3), nth(f"m{c}", g, 3))
                w = banks(f"m{c}", g, 3)
                if c == 0:
                    dve.wait_ge(h_cur_copied, g + 1)
                dve.tensor_tensor(h_cur[:, c, :, :], h_cur[:, c, :, :], w[:, :, 0:S], ALU.add).then_inc(read_of(f"m{c}", g, 3), 1)

            def lead_in():
                centre("tok", 0, 0)
                normalize("tok", 0, 0)
                dve.wait_ge(x0_ready, 1)
                centre("job", 0, 0)
                normalize("job", 0, 0)
                for c in range(CI):
                    step_size(0, 0, c)
                delta_x(0, 0, 0)

            def period(g, jj, first, last):
                for u in range(UNITS):
                    scan(g, jj, u)
                    if not (first and u == 0):
                        c_times_h(g, jj, u - 1)
                    if u % PAIRS == 1 and not (first and u == 1):
                        output(g, jj - (u == 1), (u // PAIRS - 1) % CI)
                    if u % PAIRS == 5 and u < 3 * PAIRS:
                        delta_x(g, jj, u // PAIRS + 1)
                    if u == 3 and not first:
                        residual(g, jj - 1, 0)
                        residual(g, jj - 1, 1)
                    if jj == 4 and u == 5:
                        merged(g, 0)
                        merged(g, 1)
                    if jj == 3 and not last:
                        if u == 6:
                            centre("tok", g, 4)
                        if u == 9:
                            normalize("tok", g, 4)
                    if last:
                        continue
                    if u == 10:
                        centre("job", g, jj + 1)
                    if u == 13:
                        normalize("job", g, jj + 1)
                    if u in (26, 28, 30):
                        step_size(g, jj + 1, (u - 26) // 2)
                    if u == 29:
                        delta_x(g, jj + 1, 0)
                if not last:
                    step_size(g, jj + 1, 3)

            def tail(g):
                c_times_h(g, 3, UNITS - 1)
                output(g, 3, 3)
                residual(g, 3, 0)
                residual(g, 3, 1)
                merged(g, 0)
                merged(g, 1)

            run(dve, lead_in, period, tail)

        @block.tensor
        def _(pe):
            def product(name, g, jj, terms, rows=P, sources=()):
                w = banks(name, g, jj)
                if positive(nth(name, g, jj) - 1):
                    pe.wait_ge(read_of(name, g, jj), nth(name, g, jj) - 1)
                others = [source for source in sources if slot(source[0], g, source[1]) % 2 != slot(name, g, jj) % 2]
                if others:
                    latest, of = max(others, key=lambda source: slot(source[0], g, source[1]))
                    pe.wait_ge(read_of(latest, g, of), nth(latest, g, of))
                for b in range(NB):
                    for i, (lhs, rhs) in enumerate(terms(b)):
                        last = pe.matmul(w[0:rows, b, 0:S], lhs, rhs, start=(i == 0), stop=(i == len(terms(b)) - 1))
                last.then_inc(full_of(name, g, jj), 1)

            def tokens(g, jj):
                for n in range(8):
                    c, b, half = n // 4, n // 2 % 2, n % 2
                    name = f"t{c}"
                    w = w_ps[slot(name, g, jj) % 2]
                    pe.wait_ge(x_loaded[n % 2], (g + jj // 4) * (4 * 16) + 16 * (n // 2 + 1))
                    if n % 4 == 0 and positive(nth(name, g, jj) - 1):
                        pe.wait_ge(read_of(name, g, jj), nth(name, g, jj) - 1)
                    for f in range(4):
                        last = pe.matmul(w[:, b, 1 + half * P:1 + (half + 1) * P], x_in[:, n % 2, :, f], tok_ident[:, f, :],
                                         start=(f == 0), stop=(f == 3))
                    last.then_inc(x_used, 1)
                    if n % 4 == 3:
                        pe.wait_ge(x_used, g * 8 + 8 * (jj // 4) + n + 1)
                        pe.sem_inc(full_of(name, g, jj), 1)

            def mean(kind, g, jj):
                x = h_next if kind == "tok" else stream(jj)
                sources = ()
                if kind == "tok":
                    sources = ("t0", jj), ("t1", jj)
                elif jj % 4 == 0:
                    pe.wait_ge(x0_ready, g + (jj // 4 + 1))
                elif jj % 4 == 1:
                    pe.wait_ge(x_b_copied, g + (jj // 4 + 1))
                else:
                    sources = ("o0", jj - 2), ("o1", jj - 2)
                product("tmean" if kind == "tok" else "mean", g, jj,
                        lambda b: [(mean_w[:, :], x[:, c, b, :]) for c in range(CM)], sources=sources)

            def variance(kind, g, jj):
                pe.wait_ge(squared, g * 5 + (norms[kind, jj] + 1))
                product("tvar" if kind == "tok" else "var", g, jj,
                        lambda b: [(mean_w[:, :], sq[:, c, b, :]) for c in range(CM)])

            def conv_in(g, jj, c):
                if c == 0:
                    pe.wait_ge(xn_ready, job_count(g, jj, 1, 1))
                    pe.wait_ge(in_w_loaded, job_count(g, jj, 5 * 16, 5 * 16))
                product(f"xs{c}", g, jj, lambda b: [(in_w[:, m, c * P:(c + 1) * P], xn[:, m, b, :]) for m in range(CM)])

            def conv(g, jj, c):
                pe.wait_ge(diag_ready, job_count(g, jj, CI, c + 1))
                product(f"cv{c}", g, jj,
                        lambda b: [(conv_diag[:, c % 2, tap, :], xs_pad[:, c % 2, b, tap:tap + S]) for tap in range(KW)],
                        sources=[(f"xs{c}", jj)])

            def projections(g, jj):
                product("xp", g, jj, lambda b: [(xp_w[:, c, :], xc[:, jj % 2, c, b, :]) for c in range(CI)],
                        rows=RNK + 2 * NST, sources=[("cv2", jj), ("cv3", jj)])

            def step_input(g, jj, c):
                product(f"dt{c}", g, jj, lambda b: [(dt_w[:, c * P:(c + 1) * P], dtbc[0:RNK, b, :])], sources=[("xp", jj)])

            def gates(g, jj):
                for c in range(CI):
                    lo = DI + c * P
                    product(f"z{c}", g, jj, lambda b: [(in_w[:, m, lo:lo + P], xn[:, m, b, :]) for m in range(CM)])

            def out_projection(g, jj):
                pe.wait_ge(yz_ready, job_count(g, jj, CI, CI))
                pe.wait_ge(out_w_loaded, job_count(g, jj, 16, 16))
                for j in range(CM):
                    product(f"o{j}", g, jj, lambda b: [(out_w[:, c, j * P:(j + 1) * P], sz[:, c, b, :]) for c in range(CI)])

            def merge(g):
                for j in range(CM):
                    cols = slice(j * P, (j + 1) * P)
                    product(f"m{j}", g, 3, lambda b: [(merge_w[:, c, cols], o_f[:, c, b, :]) for c in range(CM)]
                            + [(merge_w[:, CM + c, cols], x_b[:, c, b, ::-1]) for c in range(CM)],
                            sources=[("o0", 3), ("o1", 3)])

            def add_states(g, jj, u):
                jj, u = on(jj, u)
                c, n = u // PAIRS, u % PAIRS
                if n == 0:
                    if positive(job_count(g, jj, CI, c - 1)):
                        pe.wait_ge(y_read, job_count(g, jj, CI, c - 1))
                pe.wait_ge(c_done[u % 2], job_count(g, jj, UNITS // 2, u // 2 + 1))
                for i in range(NU):
                    for b in range(NB):
                        last = pe.matmul(y_ps[c % 2][:, b, 0:S], ident[:, :], hb[:, u % NHB, i, b, :],
                                         start=(n == 0 and i == 0), stop=(n == PAIRS - 1 and i == NU - 1))
                last.then_inc(y_added, 1)

            def lead_in():
                pe.wait_ge(consts_loaded, 16 * n_const_dmas)
                pe.wait_ge(zeros_set, 6)
                pe.wait_ge(ident_set, 2)
                for c in range(CI):
                    last = pe.matmul(w_ps[1][:, 0, 0:5], tok_mean[:, :], tok_w[:, c, :], start=(c == 0), stop=(c == CI - 1))
                last.then_inc(setup_pe, 1)
                pe.wait_ge(setup_act, 7)
                tokens(0, 0)
                mean("tok", 0, 0)
                variance("tok", 0, 0)
                mean("job", 0, 0)
                variance("job", 0, 0)
                conv_in(0, 0, 0)
                conv_in(0, 0, 1)
                conv(0, 0, 0)
                conv_in(0, 0, 2)
                conv(0, 0, 1)
                conv_in(0, 0, 3)
                conv(0, 0, 2)
                conv(0, 0, 3)
                projections(0, 0)
                for c in range(CI):
                    step_input(0, 0, c)

            def period(g, jj, first, last):
                for u in range(UNITS):
                    if u == 3 and not first:
                        out_projection(g, jj - 1)
                    if jj == 4 and u == 5:
                        merge(g)
                    if jj == 3 and not last:
                        if u == 4:
                            tokens(g, 4)
                        if u == 6:
                            mean("tok", g, 4)
                        if u == 8:
                            variance("tok", g, 4)
                    if u == 4 + 3 * (jj == 4) + 5 * (jj == 3):
                        gates(g, jj)
                    if not last:
                        if u == 10:
                            mean("job", g, jj + 1)
                        if u == 12:
                            variance("job", g, jj + 1)
                        if u == 14:
                            conv_in(g, jj + 1, 0)
                        if u == 15:
                            conv_in(g, jj + 1, 1)
                        if u == 16:
                            conv(g, jj + 1, 0)
                            conv_in(g, jj + 1, 2)
                        if u == 17:
                            conv(g, jj + 1, 1)
                            conv_in(g, jj + 1, 3)
                        if u == 18:
                            conv(g, jj + 1, 2)
                        if u == 19:
                            conv(g, jj + 1, 3)
                        if u == 21:
                            projections(g, jj + 1)
                        if u in (25, 27, 29):
                            step_input(g, jj + 1, (u - 25) // 2)
                        if u == 31:
                            step_input(g, jj + 1, 3)
                    if not (first and u < 2):
                        add_states(g, jj, u - 2)

            def tail(g):
                add_states(g, 3, UNITS - 2)
                add_states(g, 3, UNITS - 1)
                out_projection(g, 3)
                merge(g)

            run(pe, lead_in, period, tail)


QT = 86
TILES = [(0, 86), (86, 86), (172, 85)]
GATE_TILES = (0, 128, 129)
NE, EH2 = 4, 64
HID = 1024
HC = HID // P
KEPT = 127


def tail_phase(nc, a, h_mid, out):
    f_slots = ["mean", "var", "s1_0", "s1_1", "logits", "e1_0", "e1_1", "e1_2", "e1_3", "s2", "gates_t", "e2_0", "e2_1",
               "gates_0", "gates_1", "out_0", "out_1"]
    a_slots = ["mean", "var", "key_0", "key_1", "value_0", "value_1", "score_0", "score_1", "turned_0", "turned_1",
               "mix_0", "mix_1"]
    r_slots = ["mean", "var", "row", "rows", "column", "hid_0", "rank", "hid_1", "hid_2", "hid_3", "hid_4", "hid_5", "hid_6",
               "hid_7", "y_0", "y_1", "out_0", "out_1"]
    order = []
    for i in range(len(r_slots)):
        order.append(("R", r_slots[i]))
        if i % 3 != 2:
            order.append(("A", a_slots[i // 3 * 2 + i % 3]))
        if i != 15:
            order.append(("F", f_slots[i - (i > 15)]))
    names = {"F": f_slots, "A": a_slots, "R": r_slots}
    LAG = {"F": 0, "A": 1, "R": 2}

    def nth(s, name, g):
        return g * len(names[s]) + (names[s].index(name) + 1)

    def positive(count):
        return not isinstance(count, int) or count > 0

    with ExitStack() as ctx:
        def sb(name, shape):
            return ctx.enter_context(nc.sbuf_tensor(name, shape, F32))

        def sem(name):
            return ctx.enter_context(nc.semaphore(name))

        ident = sb("ident2", [P, P])
        mean_w = sb("mean_w2", [P, P])
        ones = sb("ones", [P, P])
        eps_t = sb("eps_t2", [P, 1])
        earlier = sb("earlier", [P, NE, NE])
        before = sb("before", [QT, 3, S])
        pair_rows = sb("pair_rows", [NE, 2, 2, EH2])
        s_w1 = sb("s_w1", [P, CM, 256])
        s_w2 = sb("s_w2", [P, 2, P])
        s_w3 = sb("s_w3", [P, DM])
        e_w1 = sb("e_w1", [P, CM, NE, P])
        e_w2 = sb("e_w2", [P, NE, EH2])
        e_w3 = sb("e_w3", [P, 2, DM])
        g_w = sb("g_w", [P, CM, NE])
        g_b = sb("g_b", [P, NE])
        e_b1 = sb("e_b1", [P, NE])
        e_b2 = sb("e_b2", [P, 2])
        e_b3 = sb("e_b3", [NE, DM])
        s_b1 = sb("s_b1", [P, 2])
        s_b2 = sb("s_b2", [P, 1])
        s_b3 = sb("s_b3", [P, CM])
        w_q = sb("w_q", [P, CM, DM])
        w_k = sb("w_k", [P, CM, DM])
        w_v = sb("w_v", [P, CM, DM])
        qk_t = sb("qk_t", [P, CM, DM])
        v_t = sb("v_t", [P, CM, DM])
        w_r = sb("w_r", [P, CM])
        b_r = sb("b_r", [1, 1])
        w_1 = sb("w_1", [P, CM, HID])
        b_1 = sb("b_1", [P, HC])
        w_2 = sb("w_2", [P, HC, DM])
        b_2 = sb("b_2", [P, CM])
        h = {s: sb(f"h_{s}", [P, CM, NB, S]) for s in "FAR"}
        x = {s: sb(f"x_{s}", [P, CM, NB, S]) for s in "FAR"}
        sq = {s: sb(f"sq_{s}", [P, CM, NB, S]) for s in "FAR"}
        rstd = {s: sb(f"rstd_{s}", [P, NB, S]) for s in "FAR"}
        s1 = sb("s1", [P, 2, NB, S])
        s2 = sb("s2", [P, NB, S])
        e1 = sb("e1", [P, NE, NB, S])
        e2 = sb("e2", [P, 2, NB, S])
        lg = sb("lg", [P, 6, NE])
        gp = sb("gp", [P, 6, NE])
        g1 = sb("g1", [P, 6])
        g2 = sb("g2", [P, 6])
        above = sb("above", [P, 6, NE, NE])
        tied = sb("tied", [P, 6, NE, NE])
        rank = sb("rank", [P, 6, NE])
        gate = sb("gate", [P, 6, NE])
        gate_t = sb("gate_t", [NE, NB, S])
        key = sb("key", [P, CM, NB, S])
        value = sb("value", [QT, NB, 3, DM])
        prob = sb("prob", [QT, NB, 3, S])
        prob_t = sb("prob_t", [QT, NB, 3, S])
        nmax = sb("nmax", [QT, NB, 3])
        psums = sb("psums", [QT, NB, 3])
        precip = sb("precip", [QT, NB, 3])
        xh = sb("xh", [P, CM, NB, S])
        w_row = sb("w_row", [1, NB, S])
        w_rows = sb("w_rows", [P, NB, S])
        w_col = sb("w_col", [QT, NB, 3])
        ahead = sb("ahead", [QT, NB, 3, S])
        sel_w = sb("sel_w", [P, NB, S])
        hid = sb("hid", [P, HC, NB, S])
        o_sb = sb("o_sb", [QT, NB, 3, DM])

        ps = {"F": ctx.enter_context(nc.psum_tensor("ps_F", [P, 2, BANK], F32)),
              "R": ctx.enter_context(nc.psum_tensor("ps_R", [P, 2, BANK], F32)),
              "A": ctx.enter_context(nc.psum_tensor("ps_A", [P, 4, BANK], F32))}

        loaded = sem("weights_loaded")
        consts_set = sem("consts_set")
        ident_set = sem("ident2_set")
        setup_full = sem("setup_full")
        setup_read = sem("setup_read")
        full = {s: sem(f"full_{s}") for s in "FAR"}
        read = {s: sem(f"read_{s}") for s in "FAR"}
        squared = {s: sem(f"squared_{s}") for s in "FAR"}
        rstd_ready = {s: sem(f"rstd_ready_{s}") for s in "FAR"}
        x_ready = {s: sem(f"x_ready_{s}") for s in "FAR"}
        h_loaded = sem("h_loaded")
        router = sem("router")
        router_exp = sem("router_exp")
        gates_ready = sem("gates_ready")
        max_ready = sem("max_ready")
        exps_ready = sem("exps_ready")
        recips_ready = sem("recips_ready")
        probs_ready = sem("probs_ready")
        ahead_part = sem("ahead_part")
        ahead_ready = sem("ahead_ready")
        xh_ready = sem("xh_ready")
        scaled = sem("scaled")
        o_ready = sem("o_ready")
        stored = [sem(f"stored_{b}") for b in range(NB)]

        n_loads = 2 * NE + 21
        ROUTER = 15

        def run(eng, body, setup, finish):
            setup()
            for turn in (0, 1, 2):
                body(turn)
            with eng.Fori(3, GROUPS) as turn:
                body(turn)
            for turn in (GROUPS, GROUPS + 1):
                body(turn)
            finish()

        def walk(turn, slot):
            for s, name in order:
                if isinstance(turn, int) and not 0 <= turn - LAG[s] < GROUPS:
                    continue
                slot(s, name, turn - LAG[s])

        block = ctx.enter_context(nc.Block())

        @block.sync
        def _(sp):
            def load(dst, src):
                sp.dma_start(dst, src, allow_slow_non_contiguous=True).then_inc(loaded, 16)

            def load_h(g):
                if positive(nth("F", "out_1", g - 1)):
                    sp.wait_ge(read["F"], nth("F", "out_1", g - 1))
                sp.dma_start(h["F"][:, :, :, :], h_mid[:, :, bass.ds(g * NB, NB), :].rearrange("c p b s -> p c b s")
                             ).then_inc(h_loaded, 16)

            def setup():
                chunks = "(c p) n -> p c n"
                load(s_w1[:, :, :], a["L0_ffn_sW1"].rearrange(chunks, p=P))
                load(s_w2[:, :, :], a["L0_ffn_sW2"].rearrange(chunks, p=P))
                load(s_w3[:, :], a["L0_ffn_sW3"])
                for e in range(NE):
                    load(e_w1[:, :, e, :], a["L0_ffn_eW1"][e].rearrange(chunks, p=P))
                    load(e_w2[:, e, :], a["L0_ffn_eW2"][e])
                load(e_w3[:, :, :], a["L0_ffn_eW3"].rearrange("(q e) k n -> (e k) q n", e=2))
                load(g_w[:, :, :], a["L0_ffn_gW"].rearrange(chunks, p=P))
                load(g_b[:, :], a["L0_ffn_gb"].partition_broadcast(P))
                load(e_b1[:, :], a["L0_ffn_eb1"].rearrange("e p -> p e"))
                load(e_b2[:, :], a["L0_ffn_eb2"].rearrange("(q e) k -> (e k) q", e=2))
                load(e_b3[:, :], a["L0_ffn_eb3"])
                load(s_b1[:, :], a["L0_ffn_sb1"].rearrange("(c p) -> p c", p=P))
                load(s_b2[:, :], a["L0_ffn_sb2"].rearrange("(c p) -> p c", p=P))
                load(s_b3[:, :], a["L0_ffn_sb3"].rearrange("(c p) -> p c", p=P))
                for dst, name in ((w_q, "Wq"), (w_k, "Wk"), (w_v, "Wv")):
                    load(dst[:, :, :], a["L1_attn_" + name].rearrange(chunks, p=P))
                load(w_r[:, :], a["L1_ffn_wr"].rearrange("(c p) o -> p (c o)", p=P))
                load(b_r[:, :], a["L1_ffn_br"].rearrange("(a o) -> a o", a=1))
                load(w_1[:, :, :], a["L1_ffn_w1"].rearrange(chunks, p=P))
                load(b_1[:, :], a["L1_ffn_b1"].rearrange("(c p) -> p c", p=P))
                load(w_2[:, :, :], a["L1_ffn_w2"].rearrange(chunks, p=P))
                load(b_2[:, :], a["L1_ffn_b2"].rearrange("(c p) -> p c", p=P))

            def body(turn):
                def slot(s, name, g):
                    if s == "R" and name in ("out_0", "out_1"):
                        b = int(name[-1])
                        sp.wait_ge(read[s], nth(s, name, g))
                        for i, (t0, n) in enumerate(TILES):
                            sp.dma_start(out[bass.ds(g * NB + b, 1), t0:t0 + n, :].rearrange("o s d -> (o s) d"),
                                         o_sb[0:n, b, i, :]).then_inc(stored[b], 16)
                    if (s, name) == ("F", "mean"):
                        load_h(g)
                walk(turn, slot)

            def finish():
                for b in range(NB):
                    sp.wait_ge(stored[b], GROUPS * 3 * 16)

            run(sp, body, setup, finish)

        @block.gpsimd
        def _(pool):
            pool.memset(ident[:, :], 0.0).then_inc(ident_set, 1)
            pool.memset(earlier[:, :, :], 1.0).then_inc(ident_set, 1)
            pool.memset(before[:, :, :], 1.0).then_inc(ident_set, 1)
            pool.memset(pair_rows[:, :, :, :], 0.0).then_inc(ident_set, 1)
            pool.memset(mean_w[:, :], 1.0 / DM).then_inc(consts_set, 1)
            pool.memset(ones[:, :], 1.0).then_inc(consts_set, 1)
            pool.memset(eps_t[:, :], EPS).then_inc(consts_set, 1)
            pool.wait_ge(ident_set, 4)
            pool.affine_select(out=ident[:, :], in_=ident[:, :], compare_op=ALU.not_equal, fill=1.0, base=0,
                               pattern=[[-1, P]], channel_multiplier=1).then_inc(consts_set, 1)
            pool.affine_select(out=earlier[:, :, :], in_=earlier[:, :, :], compare_op=ALU.is_gt, fill=0.0, base=0,
                               pattern=[[1, NE], [-1, NE]], channel_multiplier=0).then_inc(consts_set, 1)
            pool.affine_select(out=before[:, :, :], in_=before[:, :, :], compare_op=ALU.is_gt, fill=0.0, base=0,
                               pattern=[[-QT, 3], [1, S]], channel_multiplier=-1).then_inc(consts_set, 1)
            pool.affine_select(out=pair_rows[:, :, :, :], in_=pair_rows[:, :, :, :], compare_op=ALU.not_equal, fill=1.0,
                               base=0, pattern=[[-2, 2], [-1, 2], [0, EH2]], channel_multiplier=1).then_inc(consts_set, 1)

        @block.scalar
        def _(act):
            func = nc.scalar.activation

            def setup():
                act.wait_ge(loaded, 16 * n_loads)
                act.wait_ge(consts_set, 7)
                act.wait_ge(setup_full, 1)
                func(qk_t[:, :, :], ps["A"][:, 0:CM, 0:DM], ACT.Identity)
                func(v_t[:, :, :], ps["A"][:, CM:2 * CM, 0:DM], ACT.Identity).then_inc(setup_read, 1)

            def slot(s, name, g):
                kind, _, i = name.partition("_")
                if kind == "var":
                    act.wait_ge(full[s], nth(s, name, g))
                    func(rstd[s][:, :, :], ps[s][:, 0:NB, 0:S], ACT.Ln, bias=eps_t[:, 0:1]).then_inc(read[s], 1)
                    act.wait_ge(read[s], nth(s, name, g))
                    func(rstd[s][:, :, :], rstd[s][:, :, :], ACT.Exp, scale=-0.5).then_inc(rstd_ready[s], 1)
                elif kind == "mean":
                    act.wait_ge(read[s], nth(s, name, g))
                    for c in range(CM):
                        last = func(sq[s][:, c, :, :], x[s][:, c, :, :], ACT.Square)
                    last.then_inc(squared[s], 1)
                elif (s, kind) == ("F", "s1"):
                    act.wait_ge(full[s], nth(s, name, g))
                    func(s1[:, int(i), :, :], ps[s][:, 0:NB, 0:S], ACT.Relu, bias=s_b1[:, int(i):int(i) + 1]).then_inc(read[s], 1)
                elif (s, kind) == ("F", "e1"):
                    act.wait_ge(full[s], nth(s, name, g))
                    func(e1[:, int(i), :, :], ps[s][:, 0:NB, 0:S], ACT.Relu, bias=e_b1[:, int(i):int(i) + 1]).then_inc(read[s], 1)
                    if i == "1":
                        act.wait_ge(router, g * ROUTER + 10)
                        func(gate[:, :, :], gate[:, :, :], ACT.Exp).then_inc(router_exp, 1)
                elif (s, kind) == ("F", "s2"):
                    act.wait_ge(full[s], nth(s, name, g))
                    func(s2[:, :, :], ps[s][:, 0:NB, 0:S], ACT.Relu, bias=s_b2[:, 0:1]).then_inc(read[s], 1)
                elif (s, name) == ("F", "gates_t"):
                    act.wait_ge(full[s], nth(s, name, g))
                    w = ps[s]
                    func(gate_t[:, :, :], w[0:NE, 0:NB, 0:S], ACT.Identity).then_inc(read[s], 1)
                elif (s, kind) == ("F", "e2"):
                    act.wait_ge(full[s], nth(s, name, g))
                    func(e2[:, int(i), :, :], ps[s][:, 0:NB, 0:S], ACT.Relu, bias=e_b2[:, int(i):int(i) + 1]).then_inc(read[s], 1)
                elif (s, name) == ("F", "logits"):
                    act.wait_ge(router, g * ROUTER + 2)
                    func(lg[:, :, :], lg[:, :, :], ACT.Exp).then_inc(router_exp, 1)
                elif (s, kind) == ("A", "key"):
                    act.wait_ge(full[s], nth(s, name, g))
                    func(key[:, int(i), :, :], ps[s][:, 0:NB, 0:S], ACT.Identity).then_inc(read[s], 1)
                elif (s, kind) == ("A", "value"):
                    act.wait_ge(full[s], nth(s, name, g))
                    w = ps[s]
                    func(value[0:QT, int(i), 0:2, :], w[0:QT, 0:2, 0:DM], ACT.Identity)
                    func(value[0:85, int(i), 2, :], w[0:85, 2, 0:DM], ACT.Identity).then_inc(read[s], 1)
                elif (s, kind) == ("A", "score"):
                    b = int(i)
                    act.wait_ge(max_ready, g * 2 * NB + 2 * b + 2)
                    for q, (t0, n) in enumerate(TILES):
                        last = func(prob[0:n, b, q, :], ps["A"][0:n, q, 0:S], ACT.Exp, bias=nmax[0:n, b, q:q + 1],
                                    accum_out=psums[0:n, b, q:q + 1])
                    last.then_inc(read[s], 1)
                elif (s, kind) == ("A", "turned"):
                    b = int(i)
                    act.wait_ge(full[s], nth(s, name, g))
                    w = ps[s]
                    func(prob_t[0:QT, b, 0:2, :], w[0:QT, 0:2, 0:S], ACT.Identity)
                    func(prob_t[0:85, b, 2, :], w[0:85, 2, 0:S], ACT.Identity).then_inc(read[s], 1)
                elif (s, name) == ("R", "row"):
                    act.wait_ge(full[s], nth(s, name, g))
                    w = ps[s]
                    func(w_row[:, :, :], w[0:1, :, 0:S], ACT.Identity, bias=b_r[:, 0:1]).then_inc(read[s], 1)
                elif (s, name) == ("R", "rows"):
                    act.wait_ge(full[s], nth(s, name, g))
                    func(w_rows[:, :, :], ps[s][:, 0:NB, 0:S], ACT.Identity).then_inc(read[s], 1)
                elif (s, name) == ("R", "column"):
                    act.wait_ge(full[s], nth(s, name, g))
                    w = ps[s]
                    func(w_col[0:QT, :, 0:2], w[0:QT, 0:NB, 0:2], ACT.Identity)
                    func(w_col[0:85, :, 2:3], w[0:85, 0:NB, 2:3], ACT.Identity).then_inc(read[s], 1)
                elif (s, kind) == ("R", "hid"):
                    act.wait_ge(full[s], nth(s, name, g))
                    func(hid[:, int(i), :, :], ps[s][:, 0:NB, 0:S], ACT.Gelu_apprx_tanh, bias=b_1[:, int(i):int(i) + 1]).then_inc(read[s], 1)
                elif (s, kind) == ("R", "out"):
                    b = int(i)
                    act.wait_ge(full[s], nth(s, name, g))
                    w = ps[s][:, :, :].rearrange("p b n -> p (b n)")
                    if positive(g * 3 * 16):
                        act.wait_ge(stored[b], g * 3 * 16)
                    func(o_sb[0:QT, b, 0:2, :].rearrange("p i n -> p (i n)"), w[0:QT, 0:2 * DM], ACT.Identity)
                    func(o_sb[0:85, b, 2, :], w[0:85, 2 * DM:3 * DM], ACT.Identity).then_inc(read[s], 1)

            run(act, lambda turn: walk(turn, slot), setup, lambda: None)

        @block.vector
        def _(dve):
            def norm(s, g):
                dve.wait_ge(rstd_ready[s], g + 1)
                for c in range(CM):
                    last = dve.tensor_tensor(x[s][:, c, :, :], x[s][:, c, :, :], rstd[s][:, :, :], ALU.mult)
                last.then_inc(x_ready[s], 1)

            def spread(t, n):
                return t[:, :].unsqueeze(2).to_broadcast([P, 6, n])

            def route_logits(g):
                dve.wait_ge(full["F"], nth("F", "logits", g))
                w = ps["F"]
                dve.tensor_tensor(lg[:, :, :], w[:, 0, 0:6 * NE].rearrange("p (t e) -> p t e", e=NE),
                                  g_b[:, :].unsqueeze(1).to_broadcast([P, 6, NE]), ALU.add).then_inc(read["F"], 1)
                dve.wait_ge(read["F"], nth("F", "logits", g))
                dve.tensor_reduce(g1[:, :], lg[:, :, :], AX.X, ALU.max).then_inc(router, 1)
                dve.wait_ge(router, g * ROUTER + 1)
                dve.tensor_tensor(lg[:, :, :], lg[:, :, :], spread(g1, NE), ALU.subtract).then_inc(router, 1)

            def route_ranks(g):
                dve.wait_ge(router_exp, g * 2 + 1)
                dve.tensor_reduce(g1[:, :], lg[:, :, :], AX.X, ALU.add).then_inc(router, 1)
                dve.wait_ge(router, g * ROUTER + 3)
                dve.reciprocal(g2[:, :], g1[:, :]).then_inc(router, 1)
                dve.wait_ge(router, g * ROUTER + 4)
                dve.tensor_tensor(gp[:, :, :], lg[:, :, :], spread(g2, NE), ALU.mult).then_inc(router, 1)
                dve.wait_ge(router, g * ROUTER + 5)
                each, other = (gp[:, :, :].unsqueeze(d).to_broadcast([P, 6, NE, NE]) for d in (3, 2))
                dve.tensor_tensor(tied[:, :, :, :], other, each, ALU.is_equal).then_inc(router, 1)
                dve.tensor_tensor(above[:, :, :, :], other, each, ALU.is_gt).then_inc(router, 1)
                dve.tensor_reduce(g1[:, :], gp[:, :, :], AX.X, ALU.max).then_inc(router, 1)
                dve.wait_ge(router, g * ROUTER + 8)
                flat = tied[:, :, :, :].rearrange("p t e j -> p t (e j)")
                dve.tensor_tensor(flat, flat, earlier[:, :, :].rearrange("p e j -> p (e j)").unsqueeze(1)
                                  .to_broadcast([P, 6, NE * NE]), ALU.mult).then_inc(router, 1)
                dve.tensor_tensor(gate[:, :, :], gp[:, :, :], spread(g1, NE), ALU.subtract).then_inc(router, 1)
                dve.wait_ge(router, g * ROUTER + 10)
                dve.tensor_tensor(above[:, :, :, :], above[:, :, :, :], tied[:, :, :, :], ALU.add).then_inc(router, 1)
                dve.wait_ge(router, g * ROUTER + 11)
                dve.tensor_reduce(rank[:, :, :], above[:, :, :, :], AX.X, ALU.add).then_inc(router, 1)
                dve.wait_ge(router, g * ROUTER + 12)

            def route_gates(g):
                dve.wait_ge(router_exp, g * 2 + 2)
                dve.scalar_tensor_tensor(out=gate[:, :, :], in0=rank[:, :, :], scalar=2.0, in1=gate[:, :, :],
                                         op0=ALU.is_lt, op1=ALU.mult).then_inc(router, 1)
                dve.wait_ge(router, g * ROUTER + 13)
                dve.tensor_reduce(g1[:, :], gate[:, :, :], AX.X, ALU.add).then_inc(router, 1)
                dve.wait_ge(router, g * ROUTER + 14)
                dve.reciprocal(g2[:, :], g1[:, :]).then_inc(router, 1)
                dve.wait_ge(router, g * ROUTER + 15)
                dve.tensor_tensor(gate[:, :, :], gate[:, :, :], spread(g2, NE), ALU.mult).then_inc(gates_ready, 1)

            def slot(s, name, g):
                kind, _, i = name.partition("_")
                if kind == "mean":
                    dve.wait_ge(full[s], nth(s, name, g))
                    w = ps[s]
                    for c in range(CM):
                        last = dve.tensor_tensor(x[s][:, c, :, :], h[s][:, c, :, :], w[:, 0:NB, 0:S], ALU.subtract)
                    last.then_inc(read[s], 1)
                elif kind == "var":
                    norm(s, g)
                    if s == "R":
                        dve.wait_ge(x_ready[s], g + 1)
                        for c in range(CM):
                            last = dve.tensor_tensor(xh[:, c, :, :], x[s][:, c, :, :], h[s][:, c, :, :], ALU.add)
                        last.then_inc(xh_ready, 1)
                elif (s, name) == ("F", "logits"):
                    route_logits(g)
                elif (s, name) == ("F", "e1_0"):
                    route_ranks(g)
                elif (s, name) == ("F", "e1_2"):
                    route_gates(g)
                elif (s, kind) == ("F", "gates") and i != "t":
                    dve.wait_ge(full[s], nth(s, name, g))
                    w = ps[s]
                    dve.tensor_tensor(e2[:, int(i), :, :], e2[:, int(i), :, :], w[:, 0:NB, 0:S], ALU.mult).then_inc(read[s], 1)
                elif (s, kind) == ("F", "out"):
                    c = int(i)
                    dve.wait_ge(full[s], nth(s, name, g))
                    w = ps[s]
                    if c == 0:
                        if positive(nth("A", "mix_1", g - 1)):
                            dve.wait_ge(read["A"], nth("A", "mix_1", g - 1))
                    dve.scalar_tensor_tensor(out=h["A"][:, c, :, :], in0=w[:, 0:NB, 0:S], scalar=s_b3[:, c:c + 1],
                                             in1=h["F"][:, c, :, :], op0=ALU.add, op1=ALU.add).then_inc(read[s], 1)
                elif (s, kind) == ("A", "score"):
                    b = int(i)
                    dve.wait_ge(full[s], nth(s, name, g))
                    w = ps[s]
                    dve.tensor_reduce(nmax[0:QT, b, 0:2], w[0:QT, 0:2, 0:S], AX.X, ALU.max, negate=True).then_inc(max_ready, 1)
                    dve.tensor_reduce(nmax[0:85, b, 2:3], w[0:85, 2, 0:S], AX.X, ALU.max, negate=True).then_inc(max_ready, 1)
                    dve.wait_ge(read[s], nth(s, name, g))
                    dve.reciprocal(precip[0:QT, b, 0:2], psums[0:QT, b, 0:2])
                    dve.reciprocal(precip[0:85, b, 2:3], psums[0:85, b, 2:3]).then_inc(recips_ready, 1)
                    dve.wait_ge(recips_ready, g * NB + b + 1)
                    for q, (t0, n) in enumerate(TILES):
                        last = dve.tensor_scalar(prob[0:n, b, q, :], prob[0:n, b, q, :], precip[0:n, b, q:q + 1], DM ** -0.5,
                                                 ALU.mult, ALU.mult)
                    last.then_inc(probs_ready, 1)
                elif (s, kind) == ("A", "mix"):
                    b = int(i)
                    dve.wait_ge(full[s], nth(s, name, g))
                    w = ps[s]
                    if b == 0:
                        if positive(g):
                            dve.wait_ge(xh_ready, g)
                    dve.tensor_tensor(h["R"][:, :, b, :], h["A"][:, :, b, :], w[:, 0:CM, 0:S], ALU.add).then_inc(read[s], 1)
                elif (s, name) == ("R", "column"):
                    dve.wait_ge(read[s], nth(s, name, g))
                    for b in range(NB):
                        for t, (t0, n) in enumerate(TILES):
                            last = dve.scalar_tensor_tensor(out=ahead[0:n, b, t, :], in0=w_rows[0:n, b, :],
                                                            scalar=w_col[0:n, b, t:t + 1], in1=before[0:n, t, :],
                                                            op0=ALU.is_equal, op1=ALU.mult)
                    last.then_inc(ahead_part, 1)
                    dve.wait_ge(ahead_part, g + 1)
                    for b in range(NB):
                        for t, (t0, n) in enumerate(TILES):
                            last = dve.scalar_tensor_tensor(out=ahead[0:n, b, t, :], in0=w_rows[0:n, b, :],
                                                            scalar=w_col[0:n, b, t:t + 1], in1=ahead[0:n, b, t, :],
                                                            op0=ALU.is_lt, op1=ALU.add)
                    last.then_inc(ahead_ready, 1)
                elif (s, name) == ("R", "rank"):
                    dve.wait_ge(full[s], nth(s, name, g))
                    w = ps[s]
                    dve.scalar_tensor_tensor(out=sel_w[:, :, :], in0=w[:, 0:NB, 0:S], scalar=float(KEPT), in1=w_rows[:, :, :],
                                             op0=ALU.is_lt, op1=ALU.mult).then_inc(read[s], 1)
                elif (s, kind) == ("R", "y"):
                    c = int(i)
                    dve.wait_ge(full[s], nth(s, name, g))
                    w = ps[s]
                    dve.scalar_tensor_tensor(out=sq["R"][:, c, :, :], in0=w[:, 0:NB, 0:S], scalar=b_2[:, c:c + 1],
                                             in1=sel_w[:, :, :], op0=ALU.add, op1=ALU.mult).then_inc(read[s], 1)
                    dve.wait_ge(read[s], nth(s, name, g))
                    dve.tensor_tensor(xh[:, c, :, :], xh[:, c, :, :], sq["R"][:, c, :, :], ALU.add).then_inc(o_ready, 1)

            run(dve, lambda turn: walk(turn, slot), lambda: dve.wait_ge(loaded, 16 * n_loads), lambda: None)

        @block.tensor
        def _(pe):
            def setup():
                pe.wait_ge(loaded, 16 * n_loads)
                pe.wait_ge(consts_set, 7)
                for c in range(CM):
                    rows = slice(c * P, (c + 1) * P)
                    for e in range(CM):
                        pe.matmul(ps["A"][:, c, 0:DM], w_k[:, e, rows], w_q[:, e, :], start=(e == 0), stop=(e == CM - 1))
                    for e in range(CM):
                        last = pe.matmul(ps["A"][:, CM + c, e * P:(e + 1) * P], w_v[:, e, rows], ident[:, :], start=True, stop=True)
                last.then_inc(setup_full, 1)
                pe.wait_ge(setup_read, 1)

            def slot(s, name, g):
                kind, _, i = name.partition("_")
                w = ps[s]
                xs = x[s]
                if positive(nth(s, name, g) - 1):
                    pe.wait_ge(read[s], nth(s, name, g) - 1)

                def product(terms, rows=slice(0, P)):
                    for b in range(NB):
                        for k, (lhs, rhs) in enumerate(terms(b)):
                            last = pe.matmul(w[rows, b, 0:S], lhs, rhs, start=(k == 0), stop=(k == len(terms(b)) - 1))
                    return last

                if kind == "mean":
                    if s == "F":
                        pe.wait_ge(h_loaded, g * 16 + 16)
                    elif s == "A":
                        pe.wait_ge(read["F"], nth("F", "out_1", g))
                    else:
                        pe.wait_ge(read["A"], nth("A", "mix_1", g))
                    last = product(lambda b: [(mean_w[:, :], h[s][:, c, b, :]) for c in range(CM)])
                elif kind == "var":
                    pe.wait_ge(squared[s], g + 1)
                    last = product(lambda b: [(mean_w[:, :], sq[s][:, c, b, :]) for c in range(CM)])
                elif s == "F":
                    if name == "s1_0":
                        pe.wait_ge(x_ready[s], g + 1)
                    if kind == "s1":
                        cols = slice(int(i) * P, (int(i) + 1) * P)
                        last = product(lambda b: [(s_w1[:, c, cols], xs[:, c, b, :]) for c in range(CM)])
                    elif kind == "e1":
                        last = product(lambda b: [(e_w1[:, c, int(i), :], xs[:, c, b, :]) for c in range(CM)])
                    elif kind == "s2":
                        last = product(lambda b: [(s_w2[:, c, :], s1[:, c, b, :]) for c in range(2)])
                    elif kind == "logits":
                        for t in range(6):
                            b, t0 = t // 3, GATE_TILES[t % 3]
                            for c in range(CM):
                                last = pe.matmul(w[:, 0, NE * t:NE * (t + 1)], xs[:, c, b, t0:t0 + P], g_w[:, c, :],
                                                 start=(c == 0), stop=(c == CM - 1))
                    elif name == "gates_t":
                        pe.wait_ge(gates_ready, g + 1)
                        for t in (0, 1, 2, 3, 4, 5):
                            b, t0 = t // 3, GATE_TILES[t % 3]
                            last = pe.matmul(w[0:NE, b, t0:t0 + P], gate[:, t, :], ident[:, :], start=True, stop=True)
                    elif kind == "e2":
                        for b in range(NB):
                            for k in range(2):
                                e = 2 * int(i) + k
                                last = pe.matmul(w[k * EH2:(k + 1) * EH2, b, 0:S], e_w2[:, e, :], e1[:, e, b, :],
                                                 start=True, stop=True)
                    elif kind == "gates":
                        last = product(lambda b: [(pair_rows[:, int(i), :, :].rearrange("p e k -> p (e k)"), gate_t[:, b, :])])
                    elif kind == "out":
                        cols = slice(int(i) * P, (int(i) + 1) * P)
                        last = product(lambda b: [(s_w3[:, cols], s2[:, b, :])]
                                       + [(e_w3[:, q, cols], e2[:, q, b, :]) for q in range(2)]
                                       + [(e_b3[:, cols], gate_t[:, b, :])])
                elif s == "A":
                    if name == "key_0":
                        pe.wait_ge(x_ready[s], g + 1)
                    if kind == "key":
                        cols = slice(int(i) * P, (int(i) + 1) * P)
                        last = product(lambda b: [(qk_t[:, c, cols], xs[:, c, b, :]) for c in range(CM)])
                    elif kind == "value":
                        b = int(i)
                        for t, (t0, n) in enumerate(TILES):
                            for c in range(CM):
                                last = pe.matmul(w[0:n, t, 0:DM], xs[:, c, b, t0:t0 + n], v_t[:, c, :],
                                                 start=(c == 0), stop=(c == CM - 1))
                    elif kind == "score":
                        b = int(i)
                        for t, (t0, n) in enumerate(TILES):
                            for c in range(CM):
                                last = pe.matmul(w[0:n, t, 0:S], xs[:, c, b, t0:t0 + n], key[:, c, b, :],
                                                 start=(c == 0), stop=(c == CM - 1))
                    elif kind == "turned":
                        b = int(i)
                        pe.wait_ge(probs_ready, g * NB + b + 1)
                        for k, (k0, nk) in enumerate(TILES):
                            for q, (q0, nq) in enumerate(TILES):
                                last = pe.matmul(w[0:nk, k, q0:q0 + nq], prob[0:nq, b, q, k0:k0 + nk], ident[0:nq, 0:nq],
                                                 start=True, stop=True)
                    elif kind == "mix":
                        b = int(i)
                        for c in range(CM):
                            for k, (k0, nk) in enumerate(TILES):
                                last = pe.matmul(w[:, c, 0:S], value[0:nk, b, k, c * P:(c + 1) * P], prob_t[0:nk, b, k, :],
                                                 start=(k == 0), stop=(k == 2))
                else:
                    if name == "row":
                        pe.wait_ge(x_ready[s], g + 1)
                        last = product(lambda b: [(w_r[:, c:c + 1], xs[:, c, b, :]) for c in range(CM)], rows=slice(0, 1))
                    elif name == "rows":
                        last = product(lambda b: [(ones[0:1, :], w_row[:, b, :])])
                    elif name == "column":
                        for b in range(NB):
                            for t, (t0, n) in enumerate(TILES):
                                last = pe.matmul(w[0:n, b, t:t + 1], w_row[:, b, t0:t0 + n], ones[0:1, 0:1], start=True, stop=True)
                    elif name == "rank":
                        pe.wait_ge(ahead_ready, g + 1)
                        last = product(lambda b: [(ones[0:n, :], ahead[0:n, b, t, :]) for t, (t0, n) in enumerate(TILES)])
                    elif kind == "hid":
                        cols = slice(int(i) * P, (int(i) + 1) * P)
                        last = product(lambda b: [(w_1[:, c, cols], xs[:, c, b, :]) for c in range(CM)])
                    elif kind == "y":
                        cols = slice(int(i) * P, (int(i) + 1) * P)
                        last = product(lambda b: [(w_2[:, k, cols], hid[:, k, b, :]) for k in range(HC)])
                    elif kind == "out":
                        b = int(i)
                        pe.wait_ge(o_ready, g * CM + CM)
                        flat = w[:, :, :].rearrange("p b n -> p (b n)")
                        for t, (t0, n) in enumerate(TILES):
                            for c in range(CM):
                                last = pe.matmul(flat[0:n, t * DM + c * P:t * DM + (c + 1) * P], xh[:, c, b, t0:t0 + n],
                                                 ident[:, :], start=True, stop=True)
                last.then_inc(full[s], 1)

            run(pe, lambda turn: walk(turn, slot), setup, lambda: None)


INPUTS = ['x', 'cls_tok', 'L0_tok_W', 'L0_tok_b'] + ['L0_attn_' + n for n in (
    'in_w', 'conv_w', 'conv_b', 'A_log', 'xd_w', 'xB_w', 'xC_w', 'dtp_w', 'dtp_b', 'D', 'out_w', 'ln_g', 'ln_b', 'merge_w')
] + ['L0_ffn_' + n for n in ('sW1', 'sb1', 'sW2', 'sb2', 'sW3', 'sb3', 'eW1', 'eb1', 'eW2', 'eb2', 'eW3', 'eb3', 'gW', 'gb')
] + ['L1_attn_Wq', 'L1_attn_Wk', 'L1_attn_Wv'] + ['L1_ffn_' + n for n in ('wr', 'br', 'w1', 'b1', 'w2', 'b2')]


def kernel(**inputs):
    import numpy as _np
    import concourse.bacc as _bacc
    from concourse import mybir as _mybir
    from concourse.bass_utils import run_bass_kernel_spmd as _run

    nc = _bacc.Bacc("TRN2", target_bir_lowering=False, num_devices=1)
    arrays, a = {}, {}
    for name in INPUTS:
        v = _np.ascontiguousarray(inputs[name])
        arrays["in_" + name] = v
        a[name] = nc.dram_tensor("in_" + name, v.shape, _mybir.dt.from_np(v.dtype), kind="ExternalInput").ap()
    out = nc.dram_tensor("out_0", (NBATCH, S, DM), F32, kind="ExternalOutput").ap()
    h_mid = nc.dram_tensor("h_mid", (CM, P, NBATCH, S), F32, kind="Internal").ap()
    bc_dram = nc.dram_tensor("bc_dram", (2, 2 * NST, T), F32, kind="Internal").ap()
    mamba_phase(nc, a, h_mid, bc_dram)
    tail_phase(nc, a, h_mid, out)
    r = _run(nc, [arrays], core_ids=[0])
    return r.results[0]["out_0"]
```

```python
import concourse.bass as bass
from concourse import mybir
from contextlib import ExitStack

F32 = mybir.dt.float32
ALU = mybir.AluOpType
ACT = mybir.ActivationFunctionType
AX = mybir.AxisListType

P = 128
NBATCH, S, DM = 32, 257, 256
BANK = 512
NB = 2
T = NB * S
GROUPS = NBATCH // NB
CM = DM // P
DI, NST, RNK, KW = 512, 16, 32, 4
CI = DI // P
NU = 2
PAIRS = NST // NU
UNITS = CI * PAIRS
NHB, NDA = 4, 4
AHEAD = NDA - 1
BLOCK_OF_JOB = (0, 2, 1, 3)
EPS = 1e-5
LN_SLACK = 2.0 ** -23


def mamba_phase(nc, a, h_mid, bc_dram):

    norm = ["cen0", "cen1", "var"]
    conv = ["xs0", "xs1", "cv0", "cv1", "xs2", "xs3", "cv2", "cv3"]
    gates_of_job = ["z0", "z1", "z2", "z3"]

    def preparation(jj, tokens):
        steps = norm + (["t0", "t1"] if tokens else []) + conv + ["xp", "dt0", "dt1", "dt2", "dt3"]
        return [(name, 4 if name in ("t0", "t1") else jj) for name in steps]

    def one_job(jj, more):
        keys = [("tmean", 4)] if jj == 3 and more else []
        keys += [("o0", jj - 1), ("o1", jj - 1)]
        keys += [("tvar", 4)] if jj == 3 and more else []
        keys += [("m0", 3), ("m1", 3)] if jj == 4 else []
        keys += [(name, jj) for name in gates_of_job]
        return keys + (preparation(jj + 1, jj == 2 and more) if more or jj < 3 else [])

    first_keys = [(name, 0) for name in ["t0", "t1", "tmean", "tvar"]] + preparation(0, False)
    first_keys += [(name, 0) for name in gates_of_job] + preparation(1, False)
    body_keys = [key for jj in (1, 2, 3, 4) for key in one_job(jj, True)]
    final_keys = [key for jj in (1, 2, 3) for key in one_job(jj, False)] + [("o0", 3), ("o1", 3), ("m0", 3), ("m1", 3)]
    n_first, n_body = len(first_keys), len(body_keys)
    assert n_first % 2 == 0 and n_body % 2 == 0
    slots = {key: i for i, key in enumerate(first_keys + body_keys)}
    final_slots = {key: n_first + i for i, key in enumerate(final_keys)}

    def is_final(g):
        return isinstance(g, int) and g == GROUPS - 1

    def slot(name, g, jj):
        return final_slots.get((name, jj), slots.get((name, jj))) if is_final(g) else slots[name, jj]

    def gates_at(jj):
        return 8 if jj == 4 else 5

    def norm_at(jj):
        return 12 if jj == 4 else 8

    def conv_at(jj):
        return 15 if jj in (2, 4) else 14

    norms = {("tok", 0): 0, ("job", 0): 1, ("job", 1): 2}
    for key in [("job", 2), ("job", 3), ("tok", 4), ("job", 4), ("job", 5)]:
        norms[key] = len(norms)

    def job_count(g, jj, per_job, k):
        return g * (4 * per_job) + (jj * per_job + k)

    def nth(name, g, jj):
        return g * (n_body // 2) + (slot(name, g, jj) // 2 + 1)

    def positive(count):
        return not isinstance(count, int) or count > 0

    registers = {}

    def in_registers(eng, *values):
        held = []
        for i, value in enumerate(values):
            if not isinstance(value, int):
                register = registers.get((eng.engine, i)) or eng.alloc_register(f"wait_value{i}")
                registers[eng.engine, i] = register
                eng.reg_mov(register, value)
                value = register
            held.append(value)
        return held

    with ExitStack() as ctx:
        def sb(name, shape):
            return ctx.enter_context(nc.sbuf_tensor(name, shape, F32))

        def sem(name):
            return ctx.enter_context(nc.semaphore(name))

        ident = sb("ident", [P, P])
        tok_ident = sb("tok_ident", [P, 4, P])
        mean_w = sb("mean_w", [P, P])
        tok_mean = sb("tok_mean", [P, P])
        minus_centre = tok_mean
        tok_w = sb("tok_w", [P, CI, 5])
        tok_wb = sb("tok_wb", [P, 5])
        eps_t = sb("eps_t", [P, 1])
        sq_bias = sb("sq_bias", [P, 1])
        neg_a = sb("neg_a", [P, 4, CI, NST])
        conv_w = sb("conv_w", [P, 4, CI, KW])
        conv_b = sb("conv_b", [P, 4, CI])
        dtp_b = sb("dtp_b", [P, 4, CI])
        d_skip = sb("d_skip", [P, 4, CI])
        ln_g = sb("ln_g", [P, 4, CM])
        ln_b = sb("ln_b", [P, 4, CM])
        merge_w = sb("merge_w", [P, 2 * CM, DM])
        in_w = sb("in_w", [P, CM, 2 * DI])
        out_w = sb("out_w", [P, CI, DM])
        xp_w = sb("xp_w", [P, CI, RNK + 2 * NST])
        dt_w = sb("dt_w", [RNK, DI])
        x_in = sb("x_in", [P, 2, P, 4])
        h_next = sb("h_next", [P, CM, NB, S])
        h_cur = sb("h_cur", [P, CM, NB, S])
        x_f = sb("x_f", [P, CM, NB, S])
        x_b = sb("x_b", [P, CM, NB, S])
        o_f = sb("o_f", [P, CM, NB, S])
        cen = sb("cen", [P, CM, NB, S])
        sq = sb("sq", [P, CM, NB, S])
        rstd = sb("rstd", [P, NB, S])
        xn = sb("xn", [P, CM, NB, S])
        xs_pad = sb("xs_pad", [P, 2, NB, KW - 1 + S])
        diag_store = sb("diag_store", [P, NB * T])
        conv_diag = diag_store[:, 0:2 * KW * P].rearrange("p (i k n) -> p i k n", i=2, k=KW)
        skip_diag = sb("skip_diag", [P, P])
        xc = sb("xc", [P, 2, CI, NB, S])
        dtbc = sb("dtbc", [RNK + 2 * NST, NB, S])
        sp_e = diag_store[:, 0:T].rearrange("p (b s) -> p b s", b=NB), sq[:, 0, :, :]
        sp_q = diag_store[:, T:2 * T].rearrange("p (b s) -> p b s", b=NB), sq[:, 1, :, :]
        sp_l = sb("sp_l", [P, NB, S])[:, :, :], cen[:, 0, :, :]
        sp_r = rstd[:, :, :], cen[:, 1, :, :]
        delta = sb("delta", [P, CI, NB, S])
        u_buf = sb("u_buf", [P, 2, NB, S])
        decay = sb("decay", [P, NDA, NU, NB, S])
        hb = sb("hb", [P, NHB, NU, NB, S])
        b_all = sb("b_all", [P, PAIRS, NU, NB, S])
        c_all = sb("c_all", [P, PAIRS, NU, NB, S])
        sz = sb("sz", [P, CI, NB, S])

        y_ps = [ctx.enter_context(nc.psum_tensor(f"y_ps{i}", [P, NB, BANK], F32)) for i in range(2)]
        w_ps = [ctx.enter_context(nc.psum_tensor(f"w_ps{i}", [P, NB, BANK], F32)) for i in range(2)]

        consts_loaded = sem("consts_loaded")
        zeros_set = sem("zeros_set")
        ident_set = sem("ident_set")
        centre_set = sem("centre_set")
        setup_pe = sem("setup_pe")
        setup_act = sem("setup_act")
        in_w_loaded = sem("in_w_loaded")
        out_w_loaded = sem("out_w_loaded")
        x_loaded = [sem(f"x_loaded{i}") for i in range(2)]
        x_used = sem("x_used")
        work_full = [sem(f"work_full{i}") for i in range(2)]
        work_read = [sem(f"work_read{i}") for i in range(2)]
        h_cur_copied = sem("h_cur_copied")
        x0_ready = sem("x0_ready")
        x_b_copied = sem("x_b_copied")
        squared = sem("squared")
        rstd_ready = sem("rstd_ready")
        xhat_ready = sem("xhat_ready")
        xn_ready = sem("xn_ready")
        diag_ready = sem("diag_ready")
        bc_stored = sem("bc_stored")
        bc_loaded = [sem(f"bc_loaded{i}") for i in range(PAIRS)]
        sp_abs = sem("sp_abs")
        sp_exp = sem("sp_exp")
        sp_logs = sem("sp_logs")
        sp_sums = sem("sp_sums")
        delta_ready = sem("delta_ready")
        u_ready = sem("u_ready")
        decays_ready = sem("decays_ready")
        b_done = sem("b_done")
        scan_done = sem("scan_done")
        c_done = sem("c_done")
        skip_diag_ready = sem("skip_diag_ready")
        y_added = sem("y_added")
        yz_ready = sem("yz_ready")
        h_mid_stored = sem("h_mid_stored")

        n_const_dmas = CI + 1 + 1 + NB * CM + 4 * 7

        def on(jj, u):
            return jj + u // UNITS, u % UNITS

        def banks(name, g, jj):
            return w_ps[slot(name, g, jj) % 2]

        def full_of(name, g, jj):
            return work_full[slot(name, g, jj) % 2]

        def read_of(name, g, jj):
            return work_read[slot(name, g, jj) % 2]

        def stream(jj):
            return x_b if jj % 2 else x_f

        def run(eng, lead_in, period, tail):
            lead_in()
            period(0, 0, True, False)
            with eng.Fori(0, GROUPS - 1) as g:
                for jj in (1, 2, 3, 4):
                    period(g, jj, False, False)
            for jj in (1, 2, 3):
                period(GROUPS - 1, jj, False, jj == 3)
            tail(GROUPS - 1)

        block = ctx.enter_context(nc.Block())

        @block.sync
        def _(sp):
            def const(dst, src):
                sp.dma_start(dst, src, allow_slow_non_contiguous=True).then_inc(consts_loaded, 16)

            def load_weights(jj):
                k = BLOCK_OF_JOB[jj % 4]
                sp.dma_start(in_w[:, :, :], a["L0_attn_in_w"][k].rearrange("(c p) n -> p c n", p=P)).then_inc(in_w_loaded, 16)
                for name, lo, hi in (("xd_w", 0, RNK), ("xB_w", RNK, RNK + NST), ("xC_w", RNK + NST, RNK + 2 * NST)):
                    sp.dma_start(xp_w[:, :, lo:hi], a[f"L0_attn_{name}"][k].rearrange("(c p) n -> p c n", p=P),
                                 allow_slow_non_contiguous=True).then_inc(in_w_loaded, 16)
                sp.dma_start(dt_w[:, :], a["L0_attn_dtp_w"][k]).then_inc(in_w_loaded, 16)

            def load_out_w(jj):
                sp.dma_start(out_w[:, :, :], a["L0_attn_out_w"][BLOCK_OF_JOB[jj % 4]].rearrange("(c p) n -> p c n", p=P)
                             ).then_inc(out_w_loaded, 16)

            def bring_bc(g, jj):
                sp.wait_ge(read_of("xp", g, jj), nth("xp", g, jj))
                rows = bc_dram[jj % 2]
                sp.dma_start(rows, dtbc[RNK:, :, :].rearrange("r b s -> r (b s)")).then_inc(bc_stored, 16)
                for n in range(PAIRS):
                    counts = in_registers(sp, job_count(g, jj, 16, 16), job_count(g, jj - 1, UNITS, 3 * PAIRS + n + 1))
                    if n == 0:
                        sp.wait_ge(bc_stored, counts[0])
                    if positive(counts[1]):
                        sp.wait_ge(c_done, counts[1])
                    for dst, first_row in ((b_all, 0), (c_all, NST)):
                        r = first_row + NU * n
                        sp.dma_start(dst[:, n, :, :, :].rearrange("p n b s -> p (n b s)"),
                                     rows[r:r + NU, :].rearrange("r t -> (r t)").partition_broadcast(P)
                                     ).then_inc(bc_loaded[n], 16)

            def store_h(g):
                sp.wait_ge(read_of("m1", g, 3), nth("m1", g, 3))
                for c in range(CM):
                    sp.dma_start(h_mid[c, :, bass.ds(g * NB, NB), :], h_cur[:, c, :, :]).then_inc(h_mid_stored, 16)

            def lead_in():
                for c in range(CI):
                    const(tok_w[:, c, 0:4], a["L0_tok_W"][c * P:(c + 1) * P, :])
                const(tok_w[:, :, 4:5], a["L0_tok_b"].rearrange("(c p o) -> p c o", p=P, o=1))
                const(merge_w[:, :, :], a["L0_attn_merge_w"].rearrange("(c p) n -> p c n", p=P))
                cls = a["cls_tok"].rearrange("a b (c p) -> p c (a b)", p=P)
                for b in range(NB):
                    for c in range(CM):
                        const(h_next[:, c, b, 0:1], cls[:, c, :])
                for k in range(4):
                    const(neg_a[:, k, :, :], a["L0_attn_A_log"][k].rearrange("(c p) n -> p c n", p=P))
                    const(conv_w[:, k, :, :], a["L0_attn_conv_w"][k].rearrange("(c p) n -> p c n", p=P))
                    for dst, name in ((conv_b, "conv_b"), (dtp_b, "dtp_b"), (d_skip, "D"), (ln_g, "ln_g"), (ln_b, "ln_b")):
                        const(dst[:, k, :], a[f"L0_attn_{name}"][k].rearrange("(c p) -> p c", p=P))
                load_weights(0)
                bring_bc(0, 0)

            def period(g, jj, first, last):
                if not first:
                    sp.wait_ge(full_of("o1", g, jj - 1), nth("o1", g, jj - 1))
                load_out_w(jj)
                if jj == 4:
                    store_h(g)
                if not last:
                    sp.wait_ge(full_of("z3", g, jj), nth("z3", g, jj))
                    load_weights(jj + 1)
                    bring_bc(g, jj + 1)

            def tail(g):
                store_h(g)
                sp.wait_ge(h_mid_stored, GROUPS * CM * 16)

            run(sp, lead_in, period, tail)

        @block.gpsimd
        def _(pool):
            pool.memset(xs_pad[:, :, :, :], 0.0).then_inc(zeros_set, 1)
            pool.memset(decay[:, :, :, :, :], 0.0).then_inc(zeros_set, 1)
            pool.memset(mean_w[:, :], 1.0 / DM).then_inc(zeros_set, 1)
            pool.memset(tok_mean[:, :], 1.0 / DI).then_inc(zeros_set, 1)
            pool.memset(eps_t[:, :], EPS).then_inc(zeros_set, 1)
            pool.memset(sq_bias[:, :], -0.75 * 3 ** -0.5).then_inc(zeros_set, 1)
            pool.memset(ident[:, :], 0.0).then_inc(ident_set, 1)
            pool.wait_ge(ident_set, 1)
            pool.affine_select(out=ident[:, :], in_=ident[:, :], compare_op=ALU.not_equal, fill=1.0, base=0,
                               pattern=[[-1, P]], channel_multiplier=1).then_inc(ident_set, 1)

            def load_x(g, jj):
                for n in range(8):
                    c, b, half = n // 4, n // 2 % 2, n % 2
                    if positive(g * 8 + 8 * (jj // 4) + n - 1):
                        pool.wait_ge(x_used, g * 8 + 8 * (jj // 4) + n - 1)
                    src = a["x"][bass.ds(g * NB + (jj // 4 * NB + b), 1), half * P:(half + 1) * P, c * P:(c + 1) * P, :]
                    pool.dma_start(x_in[:, n % 2, :, :], src.rearrange("o i j f -> (o i) j f")).then_inc(x_loaded[n % 2], 16)

            def period(g, jj, first, last):
                if jj == 2 and not is_final(g):
                    load_x(g, 4)

            run(pool, lambda: load_x(0, 0), period, lambda g: None)

        @block.scalar
        def _(act):
            func = nc.scalar.activation

            def tokens(g, jj, c):
                act.wait_ge(full_of(f"t{c}", g, jj), nth(f"t{c}", g, jj))
                w = banks(f"t{c}", g, jj)
                func(h_next[:, c, :, 1:S], w[:, :, 1:S], ACT.Identity, bias=tok_wb[:, 4:5]).then_inc(read_of(f"t{c}", g, jj), 1)

            def copy_h(g, jj):
                act.wait_ge(read_of("t1", g, jj), nth("t1", g, jj))
                if positive((g + jj // 4) * (16 * CM)):
                    act.wait_ge(h_mid_stored, (g + jj // 4) * (16 * CM))
                func(h_cur[:, :, :, :], h_next[:, :, :, :], ACT.Identity).then_inc(h_cur_copied, 1)

            def square_tokens(g, jj):
                act.wait_ge(read_of("tmean", g, jj), nth("tmean", g, jj))
                for c in range(CM):
                    last = func(sq[:, c, :, :], cen[:, c, :, :], ACT.Square)
                last.then_inc(squared, 1)

            def centred(g, jj):
                if positive(job_count(g, jj - 1, CI, CI)):
                    act.wait_ge(delta_ready, job_count(g, jj - 1, CI, CI))
                act.wait_ge(full_of("cen0", g, jj), nth("cen0", g, jj))
                func(sq[:, 0, :, :], banks("cen0", g, jj)[:, :, 0:S], ACT.Square)
                func(cen[:, 0, :, :], banks("cen0", g, jj)[:, :, 0:S], ACT.Identity, scale=-1.0).then_inc(read_of("cen0", g, jj), 1)
                act.wait_ge(full_of("cen1", g, jj), nth("cen1", g, jj))
                func(sq[:, 1, :, :], banks("cen1", g, jj)[:, :, 0:S], ACT.Square).then_inc(squared, 1)
                func(cen[:, 1, :, :], banks("cen1", g, jj)[:, :, 0:S], ACT.Identity, scale=-1.0).then_inc(read_of("cen1", g, jj), 1)

            def inverse_deviation(kind, g, jj):
                name = "tvar" if kind == "tok" else "var"
                act.wait_ge(full_of(name, g, jj), nth(name, g, jj))
                w = banks(name, g, jj)
                func(rstd[:, :, :], w[:, :, 0:S], ACT.Ln, bias=eps_t[:, 0:1]).then_inc(read_of(name, g, jj), 1)
                act.wait_ge(read_of(name, g, jj), nth(name, g, jj))
                func(rstd[:, :, :], rstd[:, :, :], ACT.Exp, scale=-0.5).then_inc(rstd_ready, 1)

            def gain_and_bias(g, jj):
                k = BLOCK_OF_JOB[jj % 4]
                act.wait_ge(xhat_ready, job_count(g, jj, 1, 1))
                for c in range(CM):
                    last = func(xn[:, c, :, :], cen[:, c, :, :], ACT.Identity, scale=ln_g[:, k, c:c + 1],
                                bias=ln_b[:, k, c:c + 1])
                last.then_inc(xn_ready, 1)

            def start_backward(g, jj):
                act.wait_ge(x0_ready, g + jj // 4 + 1)
                if jj > 1:
                    act.wait_ge(full_of("m1", g, jj - 2), nth("m1", g, jj - 2))
                for c in range(CM):
                    last = func(x_b[:, c, :, :], x_f[:, c, :, ::-1], ACT.Identity)
                last.then_inc(x_b_copied, 1)

            def conv_input(g, jj, c):
                k = BLOCK_OF_JOB[jj % 4]
                act.wait_ge(full_of(f"xs{c}", g, jj), nth(f"xs{c}", g, jj))
                w = banks(f"xs{c}", g, jj)
                func(xs_pad[:, c % 2, :, KW - 1:], w[:, :, 0:S], ACT.Identity).then_inc(read_of(f"xs{c}", g, jj), 1)
                for tap in range(KW):
                    last = func(conv_diag[:, c % 2, tap, :], ident[:, :], ACT.Identity, scale=conv_w[:, k, c, tap:tap + 1])
                last.then_inc(diag_ready, 1)

            def conv_output(g, jj, c):
                k = BLOCK_OF_JOB[jj % 4]
                act.wait_ge(full_of(f"cv{c}", g, jj), nth(f"cv{c}", g, jj))
                w = banks(f"cv{c}", g, jj)
                if c == 0:
                    if positive(job_count(g, jj - 2, CI, CI)):
                        act.wait_ge(yz_ready, job_count(g, jj - 2, CI, CI))
                func(xc[:, jj % 2, c, :, :], w[:, :, 0:S], ACT.Silu, bias=conv_b[:, k, c:c + 1]).then_inc(read_of(f"cv{c}", g, jj), 1)

            def projections(g, jj):
                act.wait_ge(full_of("xp", g, jj), nth("xp", g, jj))
                w = banks("xp", g, jj)
                if positive(job_count(g, jj - 1, 16, 16)):
                    act.wait_ge(bc_stored, job_count(g, jj - 1, 16, 16))
                func(dtbc[:, :, :], w[0:RNK + 2 * NST, :, 0:S], ACT.Identity).then_inc(read_of("xp", g, jj), 1)

            def softplus_parts(g, jj, c):
                k = BLOCK_OF_JOB[jj % 4]
                act.wait_ge(full_of(f"dt{c}", g, jj), nth(f"dt{c}", g, jj))
                w = banks(f"dt{c}", g, jj)
                if positive(job_count(g, jj, CI, c - 1)):
                    act.wait_ge(delta_ready, job_count(g, jj, CI, c - 1))
                func(sp_e[c % 2], w[:, :, 0:S], ACT.Abs, bias=dtp_b[:, k, c:c + 1]).then_inc(sp_abs, 1)
                func(sp_r[c % 2], w[:, :, 0:S], ACT.Relu, bias=dtp_b[:, k, c:c + 1]).then_inc(read_of(f"dt{c}", g, jj), 1)
                act.wait_ge(sp_abs, job_count(g, jj, CI, c + 1))
                func(sp_e[c % 2], sp_e[c % 2], ACT.Exp, scale=-1.0).then_inc(sp_exp, 1)
                act.wait_ge(sp_exp, job_count(g, jj, CI, c + 1))
                func(sp_q[c % 2], sp_e[c % 2], ACT.Square, scale=3 ** -0.5, bias=sq_bias[:, 0:1])

            def softplus_logs(g, jj, c):
                for i in (c, c + 1):
                    func(sp_l[i % 2], sp_e[i % 2], ACT.Ln, bias=1.0).then_inc(sp_logs, 1)

            def gate(g, jj, c):
                act.wait_ge(full_of(f"z{c}", g, jj), nth(f"z{c}", g, jj))
                w = banks(f"z{c}", g, jj)
                func(sz[:, c, :, :], w[:, :, 0:S], ACT.Silu).then_inc(read_of(f"z{c}", g, jj), 1)

            def skip_weights(g, jj, c):
                jj, c = jj + c // CI, c % CI
                k = BLOCK_OF_JOB[jj % 4]
                if positive(job_count(g, jj, UNITS, PAIRS * (c - 1) + 1)):
                    act.wait_ge(y_added, job_count(g, jj, UNITS, PAIRS * (c - 1) + 1))
                func(skip_diag[:, :], ident[:, :], ACT.Identity, scale=d_skip[:, k, c:c + 1]).then_inc(skip_diag_ready, 1)

            def stream_out(g, jj, c):
                name = f"o{c}"
                act.wait_ge(full_of(name, g, jj), nth(name, g, jj))
                w = banks(name, g, jj)
                if jj % 4 == 0:
                    act.wait_ge(x_b_copied, g + jj // 4 + 1)
                dst = o_f if jj % 4 == 2 else stream(jj)
                func(dst[:, c, :, :], w[:, :, 0:S], ACT.Identity).then_inc(read_of(name, g, jj), 1)

            def decays(g, jj, u):
                jj, u = on(jj, u)
                c, n = u // PAIRS, u % PAIRS
                k = BLOCK_OF_JOB[jj % 4]
                if n == 0:
                    act.wait_ge(delta_ready, job_count(g, jj, CI, c + 1))
                if positive(job_count(g, jj, UNITS, u + 1 - NDA)):
                    act.wait_ge(scan_done, job_count(g, jj, UNITS, u + 1 - NDA))
                for i in range(NU):
                    last = func(decay[:, u % NDA, i, :, 1:S], delta[:, c, :, 1:S], ACT.Exp,
                                scale=neg_a[:, k, c, NU * n + i:NU * n + i + 1])
                last.then_inc(decays_ready, 1)

            def lead_in():
                act.wait_ge(consts_loaded, 16 * n_const_dmas)
                act.wait_ge(zeros_set, 6)
                act.wait_ge(ident_set, 2)
                func(neg_a[:, :, :, :], neg_a[:, :, :, :], ACT.Exp).then_inc(setup_act, 1)
                act.wait_ge(setup_pe, 1)
                func(tok_wb[:, :], w_ps[1][:, 0, 0:5], ACT.Identity).then_inc(setup_act, 1)
                act.wait_ge(setup_act, 2)
                func(neg_a[:, :, :, :], neg_a[:, :, :, :], ACT.Identity, scale=-1.0).then_inc(setup_act, 1)
                for f in range(4):
                    func(tok_ident[:, f, :], ident[:, :], ACT.Identity, scale=tok_wb[:, f:f + 1]).then_inc(setup_act, 1)
                tokens(0, 0, 0)
                tokens(0, 0, 1)
                copy_h(0, 0)
                square_tokens(0, 0)
                inverse_deviation("tok", 0, 0)
                prepare_front(0, 0)
                prepare_back(0, 0)
                softplus_parts(0, 0, 0)
                softplus_parts(0, 0, 1)
                softplus_logs(0, 0, 0)
                softplus_parts(0, 0, 2)
                act.wait_ge(setup_act, 7)
                skip_weights(0, 0, 0)
                for u in range(AHEAD):
                    decays(0, 0, u)

            def prepare_front(g, jj):
                centred(g, jj)
                inverse_deviation("job", g, jj)
                gain_and_bias(g, jj)

            def prepare_back(g, jj):
                for c in (0, 2):
                    conv_input(g, jj, c)
                    conv_input(g, jj, c + 1)
                    conv_output(g, jj, c)
                    conv_output(g, jj, c + 1)
                projections(g, jj)

            def period(g, jj, first, last):
                for u in range(UNITS):
                    if not (last and u + AHEAD >= UNITS):
                        decays(g, jj, u + AHEAD)
                    if u % PAIRS == 5 and not (last and u > 3 * PAIRS):
                        skip_weights(g, jj, u // PAIRS + 1)
                    if u == 0:
                        softplus_parts(g, jj, 3)
                    if u == 1:
                        softplus_logs(g, jj, 2)
                    if u in (4 + (jj == 3), 5 + (jj == 3)) and not first:
                        stream_out(g, jj - 1, u - 4 - (jj == 3))
                    if jj == 3 and not last:
                        if u == 4:
                            square_tokens(g, 4)
                        if u == 6:
                            inverse_deviation("tok", g, 4)
                    if jj == 0 and u == 6 or jj == 4 and u == 8:
                        start_backward(g, jj + 1)
                    if u in (gates_at(jj) + 2, gates_at(jj) + 4):
                        c = u - gates_at(jj) - 2
                        gate(g, jj, c)
                        gate(g, jj, c + 1)
                    if jj == 4 and u == 11:
                        copy_h(g, 4)
                    if last:
                        continue
                    if u == norm_at(jj) + 1:
                        centred(g, jj + 1)
                    if u == norm_at(jj) + 2:
                        inverse_deviation("job", g, jj + 1)
                    if u == (15 if jj == 4 else 12):
                        gain_and_bias(g, jj + 1)
                    if jj == 2 and not is_final(g) and u in (13, 15):
                        tokens(g, 4, (u - 13) // 2)
                    if u in (conv_at(jj) - (conv_at(jj) == 14), conv_at(jj) + 5):
                        c = 2 if u > conv_at(jj) else 0
                        conv_input(g, jj + 1, c)
                        conv_input(g, jj + 1, c + 1)
                    if u in (conv_at(jj) + 3, conv_at(jj) + 8):
                        c = (u - conv_at(jj) - 3) // 5 * 2
                        conv_output(g, jj + 1, c)
                        conv_output(g, jj + 1, c + 1)
                    if u == conv_at(jj) + 10:
                        projections(g, jj + 1)
                    if u in (26, 27):
                        softplus_parts(g, jj + 1, u - 26)
                    if u == 27:
                        softplus_logs(g, jj + 1, 0)
                    if u == 31:
                        softplus_parts(g, jj + 1, 2)

            def tail(g):
                stream_out(g, 3, 0)
                stream_out(g, 3, 1)

            run(act, lead_in, period, tail)

        @block.vector
        def _(dve):
            def centre(g, jj):
                dve.wait_ge(full_of("tmean", g, jj), nth("tmean", g, jj))
                w = banks("tmean", g, jj)
                for c in range(CM):
                    last = dve.tensor_tensor(cen[:, c, :, :], h_next[:, c, :, :], w[:, :, 0:S], ALU.subtract)
                last.then_inc(read_of("tmean", g, jj), 1)

            def normalize(kind, g, jj):
                i = norms[kind, jj]
                dve.wait_ge(rstd_ready, g * 5 + i + 1)
                if kind == "tok" and jj:
                    dve.wait_ge(full_of("tvar", g, jj), nth("tvar", g, jj))
                dst = x_f if kind == "tok" else cen
                for c in range(CM):
                    last = dve.tensor_tensor(dst[:, c, :, :], cen[:, c, :, :], rstd[:, :, :], ALU.mult)
                last.then_inc(x0_ready if kind == "tok" else xhat_ready, 1)

            def step_size(g, jj, c, part):
                if part == 0:
                    dve.wait_ge(sp_logs, job_count(g, jj, CI, c + 1))
                    dve.scalar_tensor_tensor(out=sp_q[c % 2], in0=sp_q[c % 2], scalar=13 / 16, in1=sp_e[c % 2],
                                             op0=ALU.add, op1=ALU.mult).then_inc(sp_sums, 1)
                elif part == 1:
                    dve.wait_ge(sp_sums, job_count(g, jj, 2 * CI, 2 * c + 1))
                    dve.scalar_tensor_tensor(out=sp_l[c % 2], in0=sp_l[c % 2], scalar=LN_SLACK, in1=sp_q[c % 2],
                                             op0=ALU.add, op1=ALU.min).then_inc(sp_sums, 1)
                else:
                    dve.wait_ge(sp_sums, job_count(g, jj, 2 * CI, 2 * c + 2))
                    if positive(job_count(g, jj - 1, UNITS, PAIRS * (c + 1))):
                        dve.wait_ge(decays_ready, job_count(g, jj - 1, UNITS, PAIRS * (c + 1)))
                    dve.tensor_tensor(delta[:, c, :, :], sp_l[c % 2], sp_r[c % 2], ALU.add).then_inc(delta_ready, 1)

            def delta_x(g, jj, c):
                dve.wait_ge(delta_ready, job_count(g, jj, CI, c + 1))
                if c == 0:
                    dve.wait_ge(read_of("cv3", g, jj), nth("cv3", g, jj))
                dve.tensor_tensor(u_buf[:, c % 2, :, :], delta[:, c, :, :], xc[:, jj % 2, c, :, :], ALU.mult).then_inc(u_ready, 1)

            def b_times_u(g, jj, u):
                jj, u = on(jj, u)
                c, n = u // PAIRS, u % PAIRS
                if c == 0:
                    dve.wait_ge(bc_loaded[n], job_count(g, jj, 32, 32))
                if n == 0:
                    dve.wait_ge(u_ready, job_count(g, jj, CI, c + 1))
                if positive(job_count(g, jj, UNITS, u + 1 - NHB)):
                    dve.wait_ge(y_added, job_count(g, jj, UNITS, u + 1 - NHB))
                dve.tensor_tensor(hb[:, u % NHB, :, :, :].rearrange("p n b s -> p n (b s)"),
                                  b_all[:, n, :, :, :].rearrange("p n b s -> p n (b s)"),
                                  u_buf[:, c % 2, :, :].rearrange("p b s -> p (b s)").unsqueeze(1).to_broadcast([P, NU, T]),
                                  ALU.mult).then_inc(b_done, 1)

            def scan(g, jj, u):
                jj, u = on(jj, u)
                dve.wait_ge(decays_ready, job_count(g, jj, UNITS, u + 1))
                dve.wait_ge(b_done, job_count(g, jj, UNITS, u + 1))
                h = hb[:, u % NHB, :, :, :].rearrange("p n b s -> p (n b s)")
                dve.tensor_tensor_scan(h, decay[:, u % NDA, :, :, :].rearrange("p n b s -> p (n b s)"), h, 0.0,
                                       ALU.mult, ALU.add).then_inc(scan_done, 1)

            def c_times_h(g, jj, u):
                jj, u = on(jj, u)
                dve.wait_ge(scan_done, job_count(g, jj, UNITS, u + 1))
                h = hb[:, u % NHB, :, :, :].rearrange("p n b s -> p (n b s)")
                dve.tensor_tensor(h, h, c_all[:, u % PAIRS, :, :, :].rearrange("p n b s -> p (n b s)"),
                                  ALU.mult).then_inc(c_done, 1)

            def output(g, jj, c):
                dve.wait_ge(y_added, job_count(g, jj, UNITS, PAIRS * (c + 1)))
                dve.wait_ge(read_of(f"z{c}", g, jj), nth(f"z{c}", g, jj))
                dve.tensor_tensor(sz[:, c, :, :], y_ps[c % 2][:, :, 0:S], sz[:, c, :, :], ALU.mult).then_inc(yz_ready, 1)

            def merged(g, c):
                dve.wait_ge(full_of(f"m{c}", g, 3), nth(f"m{c}", g, 3))
                w = banks(f"m{c}", g, 3)
                if c == 0:
                    dve.wait_ge(h_cur_copied, g + 1)
                dve.tensor_tensor(h_cur[:, c, :, :], h_cur[:, c, :, :], w[:, :, 0:S], ALU.add).then_inc(read_of(f"m{c}", g, 3), 1)

            def lead_in():
                dve.wait_ge(setup_pe, 1)
                dve.wait_ge(zeros_set, 6)
                dve.wait_ge(ident_set, 2)
                dve.tensor_tensor(minus_centre[:, :], mean_w[:, :], ident[:, :], ALU.subtract).then_inc(centre_set, 1)
                centre(0, 0)
                normalize("tok", 0, 0)
                normalize("job", 0, 0)
                for c in range(2):
                    for part in range(3):
                        step_size(0, 0, c, part)
                delta_x(0, 0, 0)
                b_times_u(0, 0, 0)

            def period(g, jj, first, last):
                for u in range(UNITS):
                    size = None
                    if u in (2, 3):
                        size = g, jj, u
                    elif u in (30, 31) and not last:
                        size = g, jj + 1, u - 30
                    scan(g, jj, u)
                    if size:
                        step_size(*size, 0)
                    if u == UNITS - 1 and not last:
                        delta_x(g, jj + 1, 0)
                    if not (last and u == UNITS - 1):
                        b_times_u(g, jj, u + 1)
                    if size:
                        step_size(*size, 1)
                    c_times_h(g, jj, u)
                    if size:
                        step_size(*size, 2)
                    if u == 1 and not first:
                        output(g, jj - 1, 3)
                    if u % PAIRS == 4 and u > PAIRS:
                        output(g, jj, u // PAIRS - 1)
                    if u % PAIRS == 5 and u < 3 * PAIRS:
                        delta_x(g, jj, u // PAIRS + 1)
                    if jj == 4 and u == 8:
                        merged(g, 0)
                        merged(g, 1)
                    if last:
                        continue
                    if jj == 3 and u == 3:
                        dve.wait_ge(delta_ready, job_count(g, jj, CI, CI))
                        centre(g, 4)
                    if jj == 3 and u == 7:
                        normalize("tok", g, 4)
                    if u == (15 if jj == 4 else 12):
                        normalize("job", g, jj + 1)

            def tail(g):
                output(g, 3, 3)
                merged(g, 0)
                merged(g, 1)

            run(dve, lead_in, period, tail)

        @block.tensor
        def _(pe):
            def product(name, g, jj, terms, rows=P, sources=(), part=range(NB)):
                w = banks(name, g, jj)
                if 0 in part and positive(nth(name, g, jj) - 1):
                    pe.wait_ge(read_of(name, g, jj), nth(name, g, jj) - 1)
                others = [source for source in sources if slot(source[0], g, source[1]) % 2 != slot(name, g, jj) % 2]
                if 0 in part and others:
                    latest, of = max(others, key=lambda source: slot(source[0], g, source[1]))
                    pe.wait_ge(read_of(latest, g, of), nth(latest, g, of))
                for b in part:
                    for i, (lhs, rhs) in enumerate(terms(b)):
                        last = pe.matmul(w[0:rows, b, 0:S], lhs, rhs, start=(i == 0), stop=(i == len(terms(b)) - 1))
                if NB - 1 in part:
                    last.then_inc(full_of(name, g, jj), 1)

            def tokens(g, jj, c, b):
                name = f"t{c}"
                w = banks(name, g, jj)
                for half in range(2):
                    n = 4 * c + 2 * b + half
                    pe.wait_ge(x_loaded[n % 2], (g + jj // 4) * (4 * 16) + 16 * (n // 2 + 1))
                    if n % 4 == 0 and positive(nth(name, g, jj) - 1):
                        pe.wait_ge(read_of(name, g, jj), nth(name, g, jj) - 1)
                    for f in range(4):
                        last = pe.matmul(w[:, b, 1 + half * P:1 + (half + 1) * P], x_in[:, n % 2, :, f], tok_ident[:, f, :],
                                         start=(f == 0), stop=(f == 3))
                    last.then_inc(x_used, 1)
                if b == NB - 1:
                    pe.wait_ge(x_used, g * 8 + 8 * (jj // 4) + n + 1)
                    pe.sem_inc(full_of(name, g, jj), 1)

            def token_mean(g, jj):
                product("tmean", g, jj, lambda b: [(mean_w[:, :], h_next[:, c, b, :]) for c in range(CM)],
                        sources=[("t0", jj), ("t1", jj)])

            def centre(g, jj):
                x = stream(jj)
                sources = ()
                if jj % 4 == 0:
                    pe.wait_ge(x0_ready, g + (jj // 4 + 1))
                elif jj % 4 == 1:
                    pe.wait_ge(x_b_copied, g + (jj // 4 + 1))
                else:
                    sources = ("o0", jj - 2), ("o1", jj - 2)
                for j in range(CM):
                    product(f"cen{j}", g, jj, lambda b: [(minus_centre[:, :] if c == j else mean_w[:, :], x[:, c, b, :])
                                                         for c in range(CM)], sources=sources)

            def variance(kind, g, jj):
                pe.wait_ge(squared, g * 5 + (norms[kind, jj] + 1))
                product("tvar" if kind == "tok" else "var", g, jj,
                        lambda b: [(mean_w[:, :], sq[:, c, b, :]) for c in range(CM)])

            def conv_in(g, jj, c):
                if c == 0:
                    pe.wait_ge(xn_ready, job_count(g, jj, 1, 1))
                    pe.wait_ge(in_w_loaded, job_count(g, jj, 5 * 16, 5 * 16))
                product(f"xs{c}", g, jj, lambda b: [(in_w[:, m, c * P:(c + 1) * P], xn[:, m, b, :]) for m in range(CM)])

            def conv(g, jj, c, part=range(NB)):
                pe.wait_ge(diag_ready, job_count(g, jj, CI, c + 1))
                product(f"cv{c}", g, jj,
                        lambda b: [(conv_diag[:, c % 2, tap, :], xs_pad[:, c % 2, b, tap:tap + S]) for tap in range(KW)],
                        sources=[(f"xs{c}", jj)], part=part)

            def projections(g, jj, part=range(NB)):
                product("xp", g, jj, lambda b: [(xp_w[:, c, :], xc[:, jj % 2, c, b, :]) for c in range(CI)],
                        rows=RNK + 2 * NST, sources=[("cv2", jj), ("cv3", jj)], part=part)

            def step_input(g, jj, c):
                product(f"dt{c}", g, jj, lambda b: [(dt_w[:, c * P:(c + 1) * P], dtbc[0:RNK, b, :])], sources=[("xp", jj)])

            def gate(g, jj, c):
                lo = DI + c * P
                product(f"z{c}", g, jj, lambda b: [(in_w[:, m, lo:lo + P], xn[:, m, b, :]) for m in range(CM)])

            def out_projection(g, jj, j, part=range(NB)):
                if j == 0:
                    pe.wait_ge(yz_ready, job_count(g, jj, CI, CI))
                    pe.wait_ge(out_w_loaded, job_count(g, jj, 16, 16))
                product(f"o{j}", g, jj, lambda b: [(out_w[:, c, j * P:(j + 1) * P], sz[:, c, b, :]) for c in range(CI)]
                        + [(ident[:, :], stream(jj)[:, j, b, :])], part=part)

            def merge(g, j):
                cols = slice(j * P, (j + 1) * P)
                product(f"m{j}", g, 3, lambda b: [(merge_w[:, c, cols], o_f[:, c, b, :]) for c in range(CM)]
                        + [(merge_w[:, CM + c, cols], x_b[:, c, b, ::-1]) for c in range(CM)],
                        sources=[("o0", 3), ("o1", 3)])

            def add_states(g, jj, u):
                jj, u = on(jj, u)
                c, n = u // PAIRS, u % PAIRS
                if n == 0:
                    if positive(job_count(g, jj, CI, c - 1)):
                        pe.wait_ge(yz_ready, job_count(g, jj, CI, c - 1))
                    pe.wait_ge(skip_diag_ready, job_count(g, jj, CI, c + 1))
                    for b in range(NB):
                        pe.matmul(y_ps[c % 2][:, b, 0:S], skip_diag[:, :], xc[:, jj % 2, c, b, :], start=True, stop=False)
                pe.wait_ge(c_done, job_count(g, jj, UNITS, u + 1))
                for i in range(NU):
                    for b in range(NB):
                        last = pe.matmul(y_ps[c % 2][:, b, 0:S], ident[:, :], hb[:, u % NHB, i, b, :],
                                         start=False, stop=(n == PAIRS - 1 and i == NU - 1))
                last.then_inc(y_added, 1)

            def lead_in():
                pe.wait_ge(consts_loaded, 16 * n_const_dmas)
                pe.wait_ge(zeros_set, 6)
                pe.wait_ge(ident_set, 2)
                for c in range(CI):
                    last = pe.matmul(w_ps[1][:, 0, 0:5], tok_mean[:, :], tok_w[:, c, :], start=(c == 0), stop=(c == CI - 1))
                last.then_inc(setup_pe, 1)
                pe.wait_ge(setup_act, 7)
                pe.wait_ge(centre_set, 1)
                for c in range(CM):
                    for b in range(NB):
                        tokens(0, 0, c, b)
                token_mean(0, 0)
                variance("tok", 0, 0)
                centre(0, 0)
                variance("job", 0, 0)
                for c in (0, 2):
                    conv_in(0, 0, c)
                    conv_in(0, 0, c + 1)
                    conv(0, 0, c)
                    conv(0, 0, c + 1)
                projections(0, 0)
                for c in range(CI):
                    step_input(0, 0, c)

            def period(g, jj, first, last):
                for u in range(UNITS):
                    if not (first and u == 0):
                        add_states(g, jj, u - 1)
                    if jj == 3 and not last and u == 1:
                        token_mean(g, 4)
                    if not first:
                        if u == 2:
                            out_projection(g, jj - 1, 0)
                        if u in (3 + (jj == 3), 4 + (jj == 3)):
                            out_projection(g, jj - 1, 1, part=[u - 3 - (jj == 3)])
                    if jj == 3 and not last and u == 5:
                        variance("tok", g, 4)
                    if jj == 4 and u in (6, 7):
                        merge(g, u - 6)
                    if gates_at(jj) <= u < gates_at(jj) + CI:
                        gate(g, jj, u - gates_at(jj))
                    if last:
                        continue
                    if u == norm_at(jj):
                        centre(g, jj + 1)
                    if u == norm_at(jj) + 2:
                        variance("job", g, jj + 1)
                    if jj == 2 and not is_final(g) and 11 <= u < 15:
                        tokens(g, 4, (u - 11) // 2, (u - 11) % 2)
                    step = u - conv_at(jj)
                    if conv_at(jj) == 14 and step < 4:
                        step += 1
                        if step in (3, 4):
                            conv(g, jj + 1, 1, part=[step - 3])
                    elif step == 3:
                        conv(g, jj + 1, 1)
                    elif step in (4, 5):
                        conv_in(g, jj + 1, step - 2)
                    elif step in (6, 7):
                        conv(g, jj + 1, 2, part=[step - 6])
                    elif step == 8:
                        conv(g, jj + 1, 3)
                    if step == 0:
                        conv_in(g, jj + 1, 0)
                        conv_in(g, jj + 1, 1)
                    elif step in (1, 2):
                        conv(g, jj + 1, 0, part=[step - 1])
                    if step in (9, 10):
                        projections(g, jj + 1, part=[step - 9])
                    if u in (26, 27, 30, 31):
                        step_input(g, jj + 1, (26, 27, 30, 31).index(u))

            def tail(g):
                add_states(g, 3, UNITS - 1)
                out_projection(g, 3, 0)
                out_projection(g, 3, 1)
                merge(g, 0)
                merge(g, 1)

            run(pe, lead_in, period, tail)


QT = 86
TILES = [(0, 86), (86, 86), (172, 85)]
GATE_TILES = (0, 128, 129)
NE, EH2 = 4, 64
HID = 1024
HC = HID // P
KEPT = 127


def tail_phase(nc, a, h_mid, out):
    turn_order = """R.mean F'.out_0 R.var F'.out_1 R.row R.rows A.mean R.hid_0 F.mean R.column A.var R.hid_1 F.var A.key_0
        R.hid_2 A.key_1 R.rank A.value_0 F.s1_0 R.hid_3 F.s1_1 A.value_1 F.logits R.hid_4 F.e1_0 A.score_0 R.hid_5 F.e1_1
        A.score_1 R.hid_6 F.e1_2 R.hid_7 F.e1_3 A.turned_0 F.s2 R.y_0 F.gates_t A.turned_1 F.e2_0 R.y_1 F.e2_1 A.mix_0
        F.gates_0 R.out_0 A.mix_1 R.out_1 F.gates_1""".split()
    LAG = {"F": 0, "F'": 1, "A": 1, "R": 2}
    order = []
    for entry in turn_order:
        stage, name = entry.split(".")
        order.append((stage[0], name, LAG[stage]))
    names = {s: [name for lag in range(3) for stage, name, l in order if stage == s and l == lag] for s in "FAR"}

    def nth(s, name, g):
        return g * len(names[s]) + (names[s].index(name) + 1)

    def positive(count):
        return not isinstance(count, int) or count > 0

    with ExitStack() as ctx:
        def sb(name, shape):
            return ctx.enter_context(nc.sbuf_tensor(name, shape, F32))

        def sem(name):
            return ctx.enter_context(nc.semaphore(name))

        ident = sb("ident2", [P, P])
        mean_w = sb("mean_w2", [P, P])
        ones = sb("ones", [P, P])
        eps_t = sb("eps_t2", [P, 1])
        earlier = sb("earlier", [P, NE, NE])
        before = sb("before", [QT, 3, S])
        pair_rows = sb("pair_rows", [NE, 2, 2, EH2])
        s_w1 = sb("s_w1", [P, CM, 256])
        s_w2 = sb("s_w2", [P, 2, P])
        s_w3 = sb("s_w3", [P, DM])
        e_w1 = sb("e_w1", [P, CM, NE, P])
        e_w2 = sb("e_w2", [P, NE, EH2])
        e_w3 = sb("e_w3", [P, 2, DM])
        g_w = sb("g_w", [P, CM, NE])
        g_b = sb("g_b", [P, NE])
        e_b1 = sb("e_b1", [P, NE])
        e_b2 = sb("e_b2", [P, 2])
        e_b3 = sb("e_b3", [NE, DM])
        s_b1 = sb("s_b1", [P, 2])
        s_b2 = sb("s_b2", [P, 1])
        s_b3 = sb("s_b3", [P, CM])
        w_q = sb("w_q", [P, CM, DM])
        w_k = sb("w_k", [P, CM, DM])
        w_v = sb("w_v", [P, CM, DM])
        qk_t = sb("qk_t", [P, CM, DM])
        v_t = sb("v_t", [P, CM, DM])
        w_r = sb("w_r", [P, CM])
        b_r = sb("b_r", [1, 1])
        w_1 = sb("w_1", [P, CM, HID])
        b_1 = sb("b_1", [P, HC])
        w_2 = sb("w_2", [P, HC, DM])
        b_2 = sb("b_2", [P, CM])
        h = {s: sb(f"h_{s}", [P, CM, NB, S]) for s in "FAR"}
        x = {s: sb(f"x_{s}", [P, CM, NB, S]) for s in "FAR"}
        sq = {s: sb(f"sq_{s}", [P, CM, NB, S]) for s in "FAR"}
        rstd = {s: sb(f"rstd_{s}", [P, NB, S]) for s in "FAR"}
        s1 = sb("s1", [P, 2, NB, S])
        s2 = sb("s2", [P, NB, S])
        e1 = sb("e1", [P, NE, NB, S])
        e2 = sb("e2", [P, 2, NB, S])
        lg = sb("lg", [P, 6, NE])
        gp = sb("gp", [P, 6, NE])
        g1 = sb("g1", [P, 6])
        g2 = sb("g2", [P, 6])
        above = sb("above", [P, 6, NE, NE])
        tied = sb("tied", [P, 6, NE, NE])
        rank = sb("rank", [P, 6, NE])
        gate = sb("gate", [P, 6, NE])
        gate_t = sb("gate_t", [NE, NB, S])
        key = sb("key", [P, CM, NB, S])
        value = sb("value", [QT, NB, 3, DM])
        prob = sb("prob", [QT, NB, 3, S])
        prob_t = sb("prob_t", [QT, NB, 3, S])
        nmax = sb("nmax", [QT, NB, 3])
        psums = sb("psums", [QT, NB, 3])
        precip = sb("precip", [QT, NB, 3])
        xh = sb("xh", [P, CM, NB, S])
        w_row = sb("w_row", [1, NB, S])
        w_rows = sb("w_rows", [P, NB, S])
        w_col = sb("w_col", [QT, NB, 3])
        ahead = sb("ahead", [QT, NB, 3, S])
        sel_w = sb("sel_w", [P, NB, S])
        hid = sb("hid", [P, HC, NB, S])
        o_sb = sb("o_sb", [QT, NB, 3, DM])

        ps = {"F": ctx.enter_context(nc.psum_tensor("ps_F", [P, 2, BANK], F32)),
              "R": ctx.enter_context(nc.psum_tensor("ps_R", [P, 2, BANK], F32)),
              "A": ctx.enter_context(nc.psum_tensor("ps_A", [P, 4, BANK], F32))}

        loaded = sem("weights_loaded")
        consts_set = sem("consts_set")
        ident_set = sem("ident2_set")
        setup_full = sem("setup_full")
        setup_read = sem("setup_read")
        full = {s: sem(f"full_{s}") for s in "FAR"}
        read = {s: sem(f"read_{s}") for s in "FAR"}
        h_summed = {s: sem(f"h_summed_{s}") for s in "FAR"}
        squares_summed = {s: sem(f"squares_summed_{s}") for s in "FAR"}
        squared = {s: sem(f"squared_{s}") for s in "FAR"}
        rstd_ready = {s: sem(f"rstd_ready_{s}") for s in "FAR"}
        x_ready = {s: sem(f"x_ready_{s}") for s in "FAR"}
        h_loaded = sem("h_loaded")
        router = sem("router")
        router_exp = sem("router_exp")
        gates_ready = sem("gates_ready")
        max_ready = sem("max_ready")
        recips_ready = sem("recips_ready")
        probs_ready = sem("probs_ready")
        ahead_part = sem("ahead_part")
        ahead_ready = sem("ahead_ready")
        xh_ready = sem("xh_ready")
        o_ready = sem("o_ready")
        stored = [sem(f"stored_{b}") for b in range(NB)]

        n_loads = 2 * NE + 21
        ROUTER = 15

        def run(eng, body, setup, finish):
            setup()
            for turn in (0, 1, 2):
                body(turn)
            with eng.Fori(3, GROUPS) as turn:
                body(turn)
            for turn in (GROUPS, GROUPS + 1):
                body(turn)
            finish()

        def walk(turn, slot):
            for s, name, lag in order:
                if isinstance(turn, int) and not 0 <= turn - lag < GROUPS:
                    continue
                slot(s, name, turn - lag)

        block = ctx.enter_context(nc.Block())

        chunks = "(c p) n -> p c n"

        @block.sync
        def _(sp):
            def load(dst, src):
                sp.dma_start(dst, src, allow_slow_non_contiguous=True).then_inc(loaded, 16)

            def load_h(g):
                if positive(nth("F", "out_1", g - 1)):
                    sp.wait_ge(read["F"], nth("F", "out_1", g - 1))
                sp.dma_start(h["F"][:, :, :, :], h_mid[:, :, bass.ds(g * NB, NB), :].rearrange("c p b s -> p c b s")
                             ).then_inc(h_loaded, 16)

            def setup():
                load(s_w1[:, :, :], a["L0_ffn_sW1"].rearrange(chunks, p=P))
                load(s_w2[:, :, :], a["L0_ffn_sW2"].rearrange(chunks, p=P))
                load(s_w3[:, :], a["L0_ffn_sW3"])
                for e in range(NE):
                    load(e_w1[:, :, e, :], a["L0_ffn_eW1"][e].rearrange(chunks, p=P))
                    load(e_w2[:, e, :], a["L0_ffn_eW2"][e])
                load(e_w3[:, :, :], a["L0_ffn_eW3"].rearrange("(q e) k n -> (e k) q n", e=2))
                load(g_w[:, :, :], a["L0_ffn_gW"].rearrange(chunks, p=P))
                load(g_b[:, :], a["L0_ffn_gb"].partition_broadcast(P))
                load(e_b1[:, :], a["L0_ffn_eb1"].rearrange("e p -> p e"))
                load(e_b2[:, :], a["L0_ffn_eb2"].rearrange("(q e) k -> (e k) q", e=2))
                load(e_b3[:, :], a["L0_ffn_eb3"])
                load(s_b1[:, :], a["L0_ffn_sb1"].rearrange("(c p) -> p c", p=P))
                load(s_b2[:, :], a["L0_ffn_sb2"].rearrange("(c p) -> p c", p=P))
                load(s_b3[:, :], a["L0_ffn_sb3"].rearrange("(c p) -> p c", p=P))

            def body(turn):
                def slot(s, name, g):
                    if s == "R" and name in ("out_0", "out_1"):
                        b = int(name[-1])
                        sp.wait_ge(read[s], nth(s, name, g))
                        for i, (t0, n) in enumerate(TILES):
                            sp.dma_start(out[bass.ds(g * NB + b, 1), t0:t0 + n, :].rearrange("o s d -> (o s) d"),
                                         o_sb[0:n, b, i, :]).then_inc(stored[b], 16)
                    if (s, name) == ("F", "mean"):
                        load_h(g)
                walk(turn, slot)

            def finish():
                for b in range(NB):
                    sp.wait_ge(stored[b], GROUPS * 3 * 16)

            run(sp, body, setup, finish)

        @block.gpsimd
        def _(pool):
            pool.memset(ident[:, :], 0.0).then_inc(ident_set, 1)
            pool.memset(earlier[:, :, :], 1.0).then_inc(ident_set, 1)
            pool.memset(before[:, :, :], 1.0).then_inc(ident_set, 1)
            pool.memset(pair_rows[:, :, :, :], 0.0).then_inc(ident_set, 1)
            pool.memset(mean_w[:, :], 1.0 / DM).then_inc(consts_set, 1)
            pool.memset(ones[:, :], 1.0).then_inc(consts_set, 1)
            pool.memset(eps_t[:, :], EPS).then_inc(consts_set, 1)
            pool.wait_ge(ident_set, 4)
            pool.affine_select(out=ident[:, :], in_=ident[:, :], compare_op=ALU.not_equal, fill=1.0, base=0,
                               pattern=[[-1, P]], channel_multiplier=1).then_inc(consts_set, 1)
            pool.affine_select(out=earlier[:, :, :], in_=earlier[:, :, :], compare_op=ALU.is_gt, fill=0.0, base=0,
                               pattern=[[1, NE], [-1, NE]], channel_multiplier=0).then_inc(consts_set, 1)
            pool.affine_select(out=before[:, :, :], in_=before[:, :, :], compare_op=ALU.is_gt, fill=0.0, base=0,
                               pattern=[[-QT, 3], [1, S]], channel_multiplier=-1).then_inc(consts_set, 1)
            pool.affine_select(out=pair_rows[:, :, :, :], in_=pair_rows[:, :, :, :], compare_op=ALU.not_equal, fill=1.0,
                               base=0, pattern=[[-2, 2], [-1, 2], [0, EH2]], channel_multiplier=1).then_inc(consts_set, 1)

            def slot(s, name, g):
                if (s, name) == ("F", "mean"):
                    pool.wait_ge(h_loaded, g * 16 + 16)
                    pool.tensor_tensor(rstd[s][:, :, :], h[s][:, 0, :, :], h[s][:, 1, :, :], ALU.add).then_inc(h_summed[s], 1)

            run(pool, lambda turn: walk(turn, slot), lambda: None, lambda: None)

        @block.scalar
        def _(act):
            func = nc.scalar.activation

            def load(dst, src):
                act.dma_start(dst, src, allow_slow_non_contiguous=True).then_inc(loaded, 16)

            def setup():
                for dst, name in ((w_q, "Wq"), (w_k, "Wk"), (w_v, "Wv")):
                    load(dst[:, :, :], a["L1_attn_" + name].rearrange(chunks, p=P))
                load(w_r[:, :], a["L1_ffn_wr"].rearrange("(c p) o -> p (c o)", p=P))
                load(b_r[:, :], a["L1_ffn_br"].rearrange("(a o) -> a o", a=1))
                load(w_1[:, :, :], a["L1_ffn_w1"].rearrange(chunks, p=P))
                load(b_1[:, :], a["L1_ffn_b1"].rearrange("(c p) -> p c", p=P))
                load(w_2[:, :, :], a["L1_ffn_w2"].rearrange(chunks, p=P))
                load(b_2[:, :], a["L1_ffn_b2"].rearrange("(c p) -> p c", p=P))
                act.wait_ge(loaded, 16 * n_loads)
                act.wait_ge(consts_set, 7)
                act.wait_ge(setup_full, 1)
                func(qk_t[:, :, :], ps["A"][:, 0:CM, 0:DM], ACT.Identity)
                func(v_t[:, :, :], ps["A"][:, CM:2 * CM, 0:DM], ACT.Identity).then_inc(setup_read, 1)

            def slot(s, name, g):
                kind, _, i = name.partition("_")
                if kind == "var":
                    act.wait_ge(full[s], nth(s, name, g))
                    func(rstd[s][:, :, :], ps[s][:, 0:NB, 0:S], ACT.Ln, bias=eps_t[:, 0:1]).then_inc(read[s], 1)
                    act.wait_ge(read[s], nth(s, name, g))
                    func(rstd[s][:, :, :], rstd[s][:, :, :], ACT.Exp, scale=-0.5).then_inc(rstd_ready[s], 1)
                elif kind == "mean":
                    act.wait_ge(read[s], nth(s, name, g))
                    for c in range(CM):
                        last = func(sq[s][:, c, :, :], x[s][:, c, :, :], ACT.Square)
                    last.then_inc(squared[s], 1)
                elif (s, kind) == ("F", "s1"):
                    act.wait_ge(full[s], nth(s, name, g))
                    func(s1[:, int(i), :, :], ps[s][:, 0:NB, 0:S], ACT.Relu, bias=s_b1[:, int(i):int(i) + 1]).then_inc(read[s], 1)
                elif (s, kind) == ("F", "e1"):
                    act.wait_ge(full[s], nth(s, name, g))
                    func(e1[:, int(i), :, :], ps[s][:, 0:NB, 0:S], ACT.Relu, bias=e_b1[:, int(i):int(i) + 1]).then_inc(read[s], 1)
                    if i == "1":
                        act.wait_ge(router, g * ROUTER + 10)
                        func(gate[:, :, :], gate[:, :, :], ACT.Exp).then_inc(router_exp, 1)
                elif (s, kind) == ("F", "s2"):
                    act.wait_ge(full[s], nth(s, name, g))
                    func(s2[:, :, :], ps[s][:, 0:NB, 0:S], ACT.Relu, bias=s_b2[:, 0:1]).then_inc(read[s], 1)
                elif (s, name) == ("F", "gates_t"):
                    act.wait_ge(full[s], nth(s, name, g))
                    w = ps[s]
                    func(gate_t[:, :, :], w[0:NE, 0:NB, 0:S], ACT.Identity).then_inc(read[s], 1)
                elif (s, kind) == ("F", "e2"):
                    act.wait_ge(full[s], nth(s, name, g))
                    func(e2[:, int(i), :, :], ps[s][:, 0:NB, 0:S], ACT.Relu, bias=e_b2[:, int(i):int(i) + 1]).then_inc(read[s], 1)
                elif (s, name) == ("F", "logits"):
                    act.wait_ge(router, g * ROUTER + 2)
                    func(lg[:, :, :], lg[:, :, :], ACT.Exp).then_inc(router_exp, 1)
                elif (s, kind) == ("A", "key"):
                    act.wait_ge(full[s], nth(s, name, g))
                    func(key[:, int(i), :, :], ps[s][:, 0:NB, 0:S], ACT.Identity).then_inc(read[s], 1)
                elif (s, kind) == ("A", "value"):
                    act.wait_ge(full[s], nth(s, name, g))
                    w = ps[s]
                    func(value[0:QT, int(i), 0:2, :], w[0:QT, 0:2, 0:DM], ACT.Identity)
                    func(value[0:85, int(i), 2, :], w[0:85, 2, 0:DM], ACT.Identity).then_inc(read[s], 1)
                elif (s, kind) == ("A", "score"):
                    b = int(i)
                    act.wait_ge(max_ready, g * 2 * NB + 2 * b + 2)
                    for q, (t0, n) in enumerate(TILES):
                        last = func(prob[0:n, b, q, :], ps["A"][0:n, q, 0:S], ACT.Exp, bias=nmax[0:n, b, q:q + 1],
                                    accum_out=psums[0:n, b, q:q + 1])
                    last.then_inc(read[s], 1)
                elif (s, kind) == ("A", "turned"):
                    b = int(i)
                    act.wait_ge(full[s], nth(s, name, g))
                    w = ps[s]
                    func(prob_t[0:QT, b, 0:2, :], w[0:QT, 0:2, 0:S], ACT.Identity)
                    func(prob_t[0:85, b, 2, :], w[0:85, 2, 0:S], ACT.Identity).then_inc(read[s], 1)
                elif (s, name) == ("R", "row"):
                    act.wait_ge(full[s], nth(s, name, g))
                    w = ps[s]
                    func(w_row[:, :, :], w[0:1, :, 0:S], ACT.Identity, bias=b_r[:, 0:1]).then_inc(read[s], 1)
                elif (s, name) == ("R", "rows"):
                    act.wait_ge(full[s], nth(s, name, g))
                    func(w_rows[:, :, :], ps[s][:, 0:NB, 0:S], ACT.Identity).then_inc(read[s], 1)
                elif (s, name) == ("R", "column"):
                    act.wait_ge(full[s], nth(s, name, g))
                    w = ps[s]
                    func(w_col[0:QT, :, 0:2], w[0:QT, 0:NB, 0:2], ACT.Identity)
                    func(w_col[0:85, :, 2:3], w[0:85, 0:NB, 2:3], ACT.Identity).then_inc(read[s], 1)
                elif (s, kind) == ("R", "hid"):
                    act.wait_ge(full[s], nth(s, name, g))
                    func(hid[:, int(i), :, :], ps[s][:, 0:NB, 0:S], ACT.Gelu_apprx_tanh, bias=b_1[:, int(i):int(i) + 1]).then_inc(read[s], 1)
                elif (s, kind) == ("R", "out"):
                    b = int(i)
                    act.wait_ge(full[s], nth(s, name, g))
                    w = ps[s][:, :, :].rearrange("p b n -> p (b n)")
                    if positive(g * 3 * 16):
                        act.wait_ge(stored[b], g * 3 * 16)
                    func(o_sb[0:QT, b, 0:2, :].rearrange("p i n -> p (i n)"), w[0:QT, 0:2 * DM], ACT.Identity)
                    func(o_sb[0:85, b, 2, :], w[0:85, 2 * DM:3 * DM], ACT.Identity).then_inc(read[s], 1)

            run(act, lambda turn: walk(turn, slot), setup, lambda: None)

        @block.vector
        def _(dve):
            def norm(s, g):
                dve.wait_ge(rstd_ready[s], g + 1)
                for c in range(CM):
                    last = dve.tensor_tensor(x[s][:, c, :, :], x[s][:, c, :, :], rstd[s][:, :, :], ALU.mult)
                last.then_inc(x_ready[s], 1)

            def sum_stream(s):
                dve.tensor_tensor(rstd[s][:, :, :], h[s][:, 0, :, :], h[s][:, 1, :, :], ALU.add).then_inc(h_summed[s], 1)

            def spread(t, n):
                return t[:, :].unsqueeze(2).to_broadcast([P, 6, n])

            def route_logits(g):
                dve.wait_ge(full["F"], nth("F", "logits", g))
                w = ps["F"]
                dve.tensor_tensor(lg[:, :, :], w[:, 0, 0:6 * NE].rearrange("p (t e) -> p t e", e=NE),
                                  g_b[:, :].unsqueeze(1).to_broadcast([P, 6, NE]), ALU.add).then_inc(read["F"], 1)
                dve.wait_ge(read["F"], nth("F", "logits", g))
                dve.tensor_reduce(g1[:, :], lg[:, :, :], AX.X, ALU.max).then_inc(router, 1)
                dve.wait_ge(router, g * ROUTER + 1)
                dve.tensor_tensor(lg[:, :, :], lg[:, :, :], spread(g1, NE), ALU.subtract).then_inc(router, 1)

            def route_ranks(g):
                dve.wait_ge(router_exp, g * 2 + 1)
                dve.tensor_reduce(g1[:, :], lg[:, :, :], AX.X, ALU.add).then_inc(router, 1)
                dve.wait_ge(router, g * ROUTER + 3)
                dve.reciprocal(g2[:, :], g1[:, :]).then_inc(router, 1)
                dve.wait_ge(router, g * ROUTER + 4)
                dve.tensor_tensor(gp[:, :, :], lg[:, :, :], spread(g2, NE), ALU.mult).then_inc(router, 1)
                dve.wait_ge(router, g * ROUTER + 5)
                each, other = (gp[:, :, :].unsqueeze(d).to_broadcast([P, 6, NE, NE]) for d in (3, 2))
                dve.tensor_tensor(tied[:, :, :, :], other, each, ALU.is_equal).then_inc(router, 1)
                dve.tensor_tensor(above[:, :, :, :], other, each, ALU.is_gt).then_inc(router, 1)
                dve.tensor_reduce(g1[:, :], gp[:, :, :], AX.X, ALU.max).then_inc(router, 1)
                dve.wait_ge(router, g * ROUTER + 8)
                flat = tied[:, :, :, :].rearrange("p t e j -> p t (e j)")
                dve.tensor_tensor(flat, flat, earlier[:, :, :].rearrange("p e j -> p (e j)").unsqueeze(1)
                                  .to_broadcast([P, 6, NE * NE]), ALU.mult).then_inc(router, 1)
                dve.tensor_tensor(gate[:, :, :], gp[:, :, :], spread(g1, NE), ALU.subtract).then_inc(router, 1)
                dve.wait_ge(router, g * ROUTER + 10)
                dve.tensor_tensor(above[:, :, :, :], above[:, :, :, :], tied[:, :, :, :], ALU.add).then_inc(router, 1)
                dve.wait_ge(router, g * ROUTER + 11)
                dve.tensor_reduce(rank[:, :, :], above[:, :, :, :], AX.X, ALU.add).then_inc(router, 1)
                dve.wait_ge(router, g * ROUTER + 12)

            def route_gates(g):
                dve.wait_ge(router_exp, g * 2 + 2)
                dve.scalar_tensor_tensor(out=gate[:, :, :], in0=rank[:, :, :], scalar=2.0, in1=gate[:, :, :],
                                         op0=ALU.is_lt, op1=ALU.mult).then_inc(router, 1)
                dve.wait_ge(router, g * ROUTER + 13)
                dve.tensor_reduce(g1[:, :], gate[:, :, :], AX.X, ALU.add).then_inc(router, 1)
                dve.wait_ge(router, g * ROUTER + 14)
                dve.reciprocal(g2[:, :], g1[:, :]).then_inc(router, 1)
                dve.wait_ge(router, g * ROUTER + 15)
                dve.tensor_tensor(gate[:, :, :], gate[:, :, :], spread(g2, NE), ALU.mult).then_inc(gates_ready, 1)

            def slot(s, name, g):
                kind, _, i = name.partition("_")
                if kind == "mean":
                    dve.wait_ge(full[s], nth(s, name, g))
                    w = ps[s]
                    for c in range(CM):
                        last = dve.tensor_tensor(x[s][:, c, :, :], h[s][:, c, :, :], w[:, 0:NB, 0:S], ALU.subtract)
                    last.then_inc(read[s], 1)
                    dve.wait_ge(squared[s], g + 1)
                    dve.tensor_tensor(sq[s][:, 0, :, :], sq[s][:, 0, :, :], sq[s][:, 1, :, :], ALU.add
                                      ).then_inc(squares_summed[s], 1)
                elif kind == "var":
                    norm(s, g)
                    if s == "R":
                        dve.wait_ge(x_ready[s], g + 1)
                        for c in range(CM):
                            last = dve.tensor_tensor(xh[:, c, :, :], x[s][:, c, :, :], h[s][:, c, :, :], ALU.add)
                        last.then_inc(xh_ready, 1)
                elif (s, name) == ("F", "logits"):
                    route_logits(g)
                elif (s, name) == ("F", "e1_0"):
                    route_ranks(g)
                elif (s, name) == ("F", "e1_2"):
                    route_gates(g)
                elif (s, kind) == ("F", "gates") and i != "t":
                    dve.wait_ge(full[s], nth(s, name, g))
                    w = ps[s]
                    dve.tensor_tensor(e2[:, int(i), :, :], e2[:, int(i), :, :], w[:, 0:NB, 0:S], ALU.mult).then_inc(read[s], 1)
                elif (s, kind) == ("F", "out"):
                    c = int(i)
                    dve.wait_ge(full[s], nth(s, name, g))
                    w = ps[s]
                    if c == 0:
                        if positive(nth("A", "mix_1", g - 1)):
                            dve.wait_ge(read["A"], nth("A", "mix_1", g - 1))
                    dve.scalar_tensor_tensor(out=h["A"][:, c, :, :], in0=w[:, 0:NB, 0:S], scalar=s_b3[:, c:c + 1],
                                             in1=h["F"][:, c, :, :], op0=ALU.add, op1=ALU.add).then_inc(read[s], 1)
                    if c == CM - 1:
                        dve.wait_ge(read[s], nth(s, name, g))
                        sum_stream("A")
                elif (s, kind) == ("A", "score"):
                    b = int(i)
                    dve.wait_ge(full[s], nth(s, name, g))
                    w = ps[s]
                    dve.tensor_reduce(nmax[0:QT, b, 0:2], w[0:QT, 0:2, 0:S], AX.X, ALU.max, negate=True).then_inc(max_ready, 1)
                    dve.tensor_reduce(nmax[0:85, b, 2:3], w[0:85, 2, 0:S], AX.X, ALU.max, negate=True).then_inc(max_ready, 1)
                    dve.wait_ge(read[s], nth(s, name, g))
                    dve.reciprocal(precip[0:QT, b, 0:2], psums[0:QT, b, 0:2])
                    dve.reciprocal(precip[0:85, b, 2:3], psums[0:85, b, 2:3]).then_inc(recips_ready, 1)
                    dve.wait_ge(recips_ready, g * NB + b + 1)
                    for q, (t0, n) in enumerate(TILES):
                        last = dve.tensor_scalar(prob[0:n, b, q, :], prob[0:n, b, q, :], precip[0:n, b, q:q + 1], DM ** -0.5,
                                                 ALU.mult, ALU.mult)
                    last.then_inc(probs_ready, 1)
                elif (s, kind) == ("A", "mix"):
                    b = int(i)
                    dve.wait_ge(full[s], nth(s, name, g))
                    w = ps[s]
                    if b == 0:
                        if positive(g):
                            dve.wait_ge(xh_ready, g)
                    dve.tensor_tensor(h["R"][:, :, b, :], h["A"][:, :, b, :], w[:, 0:CM, 0:S], ALU.add).then_inc(read[s], 1)
                    if b == NB - 1:
                        dve.wait_ge(read[s], nth(s, name, g))
                        sum_stream("R")
                elif (s, name) == ("R", "hid_1"):
                    dve.wait_ge(read[s], nth(s, "column", g))
                    for b in range(NB):
                        for t, (t0, n) in enumerate(TILES):
                            last = dve.scalar_tensor_tensor(out=ahead[0:n, b, t, :], in0=w_rows[0:n, b, :],
                                                            scalar=w_col[0:n, b, t:t + 1], in1=before[0:n, t, :],
                                                            op0=ALU.is_equal, op1=ALU.mult)
                    last.then_inc(ahead_part, 1)
                    dve.wait_ge(ahead_part, g + 1)
                    for b in range(NB):
                        for t, (t0, n) in enumerate(TILES):
                            last = dve.scalar_tensor_tensor(out=ahead[0:n, b, t, :], in0=w_rows[0:n, b, :],
                                                            scalar=w_col[0:n, b, t:t + 1], in1=ahead[0:n, b, t, :],
                                                            op0=ALU.is_lt, op1=ALU.add)
                    last.then_inc(ahead_ready, 1)
                elif (s, name) == ("R", "rank"):
                    dve.wait_ge(full[s], nth(s, name, g))
                    w = ps[s]
                    dve.scalar_tensor_tensor(out=sel_w[:, :, :], in0=w[:, 0:NB, 0:S], scalar=float(KEPT), in1=w_rows[:, :, :],
                                             op0=ALU.is_lt, op1=ALU.mult).then_inc(read[s], 1)
                elif (s, kind) == ("R", "y"):
                    c = int(i)
                    dve.wait_ge(full[s], nth(s, name, g))
                    w = ps[s]
                    dve.scalar_tensor_tensor(out=sq["R"][:, c, :, :], in0=w[:, 0:NB, 0:S], scalar=b_2[:, c:c + 1],
                                             in1=sel_w[:, :, :], op0=ALU.add, op1=ALU.mult).then_inc(read[s], 1)
                    dve.wait_ge(read[s], nth(s, name, g))
                    dve.tensor_tensor(xh[:, c, :, :], xh[:, c, :, :], sq["R"][:, c, :, :], ALU.add).then_inc(o_ready, 1)

            run(dve, lambda turn: walk(turn, slot), lambda: dve.wait_ge(loaded, 16 * n_loads), lambda: None)

        @block.tensor
        def _(pe):
            def setup():
                pe.wait_ge(loaded, 16 * n_loads)
                pe.wait_ge(consts_set, 7)
                for c in range(CM):
                    rows = slice(c * P, (c + 1) * P)
                    for e in range(CM):
                        pe.matmul(ps["A"][:, c, 0:DM], w_k[:, e, rows], w_q[:, e, :], start=(e == 0), stop=(e == CM - 1))
                    for e in range(CM):
                        last = pe.matmul(ps["A"][:, CM + c, e * P:(e + 1) * P], w_v[:, e, rows], ident[:, :], start=True, stop=True)
                last.then_inc(setup_full, 1)
                pe.wait_ge(setup_read, 1)

            def slot(s, name, g):
                kind, _, i = name.partition("_")
                w = ps[s]
                xs = x[s]
                if positive(nth(s, name, g) - 1):
                    pe.wait_ge(read[s], nth(s, name, g) - 1)

                def product(terms, rows=slice(0, P)):
                    for b in range(NB):
                        for k, (lhs, rhs) in enumerate(terms(b)):
                            last = pe.matmul(w[rows, b, 0:S], lhs, rhs, start=(k == 0), stop=(k == len(terms(b)) - 1))
                    return last

                if kind == "mean":
                    pe.wait_ge(h_summed[s], g + 1)
                    last = product(lambda b: [(mean_w[:, :], rstd[s][:, b, :])])
                elif kind == "var":
                    pe.wait_ge(squares_summed[s], g + 1)
                    last = product(lambda b: [(mean_w[:, :], sq[s][:, 0, b, :])])
                elif s == "F":
                    if name == "s1_0":
                        pe.wait_ge(x_ready[s], g + 1)
                    if kind == "s1":
                        cols = slice(int(i) * P, (int(i) + 1) * P)
                        last = product(lambda b: [(s_w1[:, c, cols], xs[:, c, b, :]) for c in range(CM)])
                    elif kind == "e1":
                        last = product(lambda b: [(e_w1[:, c, int(i), :], xs[:, c, b, :]) for c in range(CM)])
                    elif kind == "s2":
                        last = product(lambda b: [(s_w2[:, c, :], s1[:, c, b, :]) for c in range(2)])
                    elif kind == "logits":
                        for t in range(6):
                            b, t0 = t // 3, GATE_TILES[t % 3]
                            for c in range(CM):
                                last = pe.matmul(w[:, 0, NE * t:NE * (t + 1)], xs[:, c, b, t0:t0 + P], g_w[:, c, :],
                                                 start=(c == 0), stop=(c == CM - 1))
                    elif name == "gates_t":
                        pe.wait_ge(gates_ready, g + 1)
                        for t in (0, 1, 2, 3, 4, 5):
                            b, t0 = t // 3, GATE_TILES[t % 3]
                            last = pe.matmul(w[0:NE, b, t0:t0 + P], gate[:, t, :], ident[:, :], start=True, stop=True)
                    elif kind == "e2":
                        for b in range(NB):
                            for k in range(2):
                                e = 2 * int(i) + k
                                last = pe.matmul(w[k * EH2:(k + 1) * EH2, b, 0:S], e_w2[:, e, :], e1[:, e, b, :],
                                                 start=True, stop=True)
                    elif kind == "gates":
                        last = product(lambda b: [(pair_rows[:, int(i), :, :].rearrange("p e k -> p (e k)"), gate_t[:, b, :])])
                    elif kind == "out":
                        cols = slice(int(i) * P, (int(i) + 1) * P)
                        last = product(lambda b: [(s_w3[:, cols], s2[:, b, :])]
                                       + [(e_w3[:, q, cols], e2[:, q, b, :]) for q in range(2)]
                                       + [(e_b3[:, cols], gate_t[:, b, :])])
                elif s == "A":
                    if name == "key_0":
                        pe.wait_ge(x_ready[s], g + 1)
                    if kind == "key":
                        cols = slice(int(i) * P, (int(i) + 1) * P)
                        last = product(lambda b: [(qk_t[:, c, cols], xs[:, c, b, :]) for c in range(CM)])
                    elif kind == "value":
                        b = int(i)
                        for t, (t0, n) in enumerate(TILES):
                            for c in range(CM):
                                last = pe.matmul(w[0:n, t, 0:DM], xs[:, c, b, t0:t0 + n], v_t[:, c, :],
                                                 start=(c == 0), stop=(c == CM - 1))
                    elif kind == "score":
                        b = int(i)
                        for t, (t0, n) in enumerate(TILES):
                            for c in range(CM):
                                last = pe.matmul(w[0:n, t, 0:S], xs[:, c, b, t0:t0 + n], key[:, c, b, :],
                                                 start=(c == 0), stop=(c == CM - 1))
                    elif kind == "turned":
                        b = int(i)
                        pe.wait_ge(probs_ready, g * NB + b + 1)
                        for k, (k0, nk) in enumerate(TILES):
                            for q, (q0, nq) in enumerate(TILES):
                                last = pe.matmul(w[0:nk, k, q0:q0 + nq], prob[0:nq, b, q, k0:k0 + nk], ident[0:nq, 0:nq],
                                                 start=True, stop=True)
                    elif kind == "mix":
                        b = int(i)
                        for c in range(CM):
                            for k, (k0, nk) in enumerate(TILES):
                                last = pe.matmul(w[:, c, 0:S], value[0:nk, b, k, c * P:(c + 1) * P], prob_t[0:nk, b, k, :],
                                                 start=(k == 0), stop=(k == 2))
                else:
                    if name == "row":
                        pe.wait_ge(x_ready[s], g + 1)
                        last = product(lambda b: [(w_r[:, c:c + 1], xs[:, c, b, :]) for c in range(CM)], rows=slice(0, 1))
                    elif name == "rows":
                        last = product(lambda b: [(ones[0:1, :], w_row[:, b, :])])
                    elif name == "column":
                        for b in range(NB):
                            for t, (t0, n) in enumerate(TILES):
                                last = pe.matmul(w[0:n, b, t:t + 1], w_row[:, b, t0:t0 + n], ones[0:1, 0:1], start=True, stop=True)
                    elif name == "rank":
                        pe.wait_ge(ahead_ready, g + 1)
                        last = product(lambda b: [(ones[0:n, :], ahead[0:n, b, t, :]) for t, (t0, n) in enumerate(TILES)])
                    elif kind == "hid":
                        cols = slice(int(i) * P, (int(i) + 1) * P)
                        last = product(lambda b: [(w_1[:, c, cols], xs[:, c, b, :]) for c in range(CM)])
                    elif kind == "y":
                        cols = slice(int(i) * P, (int(i) + 1) * P)
                        last = product(lambda b: [(w_2[:, k, cols], hid[:, k, b, :]) for k in range(HC)])
                    elif kind == "out":
                        b = int(i)
                        pe.wait_ge(o_ready, g * CM + CM)
                        flat = w[:, :, :].rearrange("p b n -> p (b n)")
                        for t, (t0, n) in enumerate(TILES):
                            for c in range(CM):
                                last = pe.matmul(flat[0:n, t * DM + c * P:t * DM + (c + 1) * P], xh[:, c, b, t0:t0 + n],
                                                 ident[:, :], start=True, stop=True)
                last.then_inc(full[s], 1)

            run(pe, lambda turn: walk(turn, slot), setup, lambda: None)


INPUTS = ['x', 'cls_tok', 'L0_tok_W', 'L0_tok_b'] + ['L0_attn_' + n for n in (
    'in_w', 'conv_w', 'conv_b', 'A_log', 'xd_w', 'xB_w', 'xC_w', 'dtp_w', 'dtp_b', 'D', 'out_w', 'ln_g', 'ln_b', 'merge_w')
] + ['L0_ffn_' + n for n in ('sW1', 'sb1', 'sW2', 'sb2', 'sW3', 'sb3', 'eW1', 'eb1', 'eW2', 'eb2', 'eW3', 'eb3', 'gW', 'gb')
] + ['L1_attn_Wq', 'L1_attn_Wk', 'L1_attn_Wv'] + ['L1_ffn_' + n for n in ('wr', 'br', 'w1', 'b1', 'w2', 'b2')]


def kernel(**inputs):
    import numpy as _np
    import concourse.bacc as _bacc
    from concourse import mybir as _mybir
    from concourse.bass_utils import run_bass_kernel_spmd as _run

    nc = _bacc.Bacc("TRN2", target_bir_lowering=False, num_devices=1)
    arrays, a = {}, {}
    for name in INPUTS:
        v = _np.ascontiguousarray(inputs[name])
        arrays["in_" + name] = v
        a[name] = nc.dram_tensor("in_" + name, v.shape, _mybir.dt.from_np(v.dtype), kind="ExternalInput").ap()
    out = nc.dram_tensor("out_0", (NBATCH, S, DM), F32, kind="ExternalOutput").ap()
    h_mid = nc.dram_tensor("h_mid", (CM, P, NBATCH, S), F32, kind="Internal").ap()
    bc_dram = nc.dram_tensor("bc_dram", (2, 2 * NST, T), F32, kind="Internal").ap()
    mamba_phase(nc, a, h_mid, bc_dram)
    tail_phase(nc, a, h_mid, out)
    r = _run(nc, [arrays], core_ids=[0])
    return r.results[0]["out_0"]
```
